# Optimizing a Trainium2 kernel written in Bass

```python
import numpy as np
import jax
import jax.numpy as jnp

def _softmax(x, axis=-1):
    return jax.nn.softmax(x, axis=axis)

def _gelu(x):
    return jax.nn.gelu(x, approximate=True)

def _silu(x):
    return jax.nn.silu(x)

def _sigmoid(x):
    return jax.nn.sigmoid(x)

def _layernorm(x, axis=-1, eps=1e-05):
    m = jnp.mean(x, axis=axis, keepdims=True)
    v = jnp.var(x, axis=axis, keepdims=True)
    return (x - m) / jnp.sqrt(v + eps)

def _scatter_add(tgt, idx, src, axis=0):
    return tgt.at[idx].add(src)

def _segment_sum(src, seg, n):
    return jax.ops.segment_sum(src, seg, n)
kernel_name = 'mk_metaformer_d1_conv_nhwc512_r4_fe1062'

def setup_inputs(seed: int=0):
    np.random.seed(seed)
    _w = jnp.asarray

    def _rec_inputs():
        import jax
        import jax.numpy as jnp
        _gk = jax.random.key(seed)
        x = -0.000125 + 0.9999 * jax.random.normal(jax.random.fold_in(_gk, 1), (16, 16, 16, 128), jnp.float32)
        return x
    x = _rec_inputs()

    def _L0_conv_setup():
        import jax, jax.numpy as jnp
        import numpy as np
        B, H, W, C = (16, 16, 16, 128)
        DIM, VDIM = (64, 64)
        key = jax.random.key(seed)
        ks = jax.random.split(key, 5)
        s = 0.02
        return {'x': jax.random.normal(ks[0], (B, H, W, C), jnp.float32), 'Wq': jax.random.normal(ks[1], (C, DIM), jnp.float32) * s, 'bq': jnp.zeros((DIM,), jnp.float32), 'Wk': jax.random.normal(ks[2], (C, VDIM), jnp.float32) * s, 'bk': jnp.zeros((VDIM,), jnp.float32), 'Wv': jax.random.normal(ks[3], (C, VDIM), jnp.float32) * s, 'bv': jnp.zeros((VDIM,), jnp.float32), 'Wr': jax.random.normal(ks[4], (DIM, C), jnp.float32) * s, 'br': jnp.zeros((C,), jnp.float32)}
    _L0_conv_all = _L0_conv_setup()
    _L0_conv_in = {k: v for k, v in _L0_conv_all.items() if k in ('Wq', 'bq', 'Wk', 'bk', 'Wv', 'bv', 'Wr', 'br')}
    del _L0_conv_all

    def _L0_ffn_setup():
        import jax, jax.numpy as jnp
        import numpy as np
        NUM_EXPERTS = 8
        TOP_K = 2
        key = jax.random.key(seed)
        ks = jax.random.split(key, 6)
        B, S, D, F, E = (2, 512, 128, 384, NUM_EXPERTS)
        scale = 0.02
        return {'x': jax.random.normal(ks[0], (B, S, D), dtype=jnp.float32), 'Wg': jax.random.normal(ks[1], (D, E), dtype=jnp.float32) * scale, 'W1': jax.random.normal(ks[2], (E, D, F), dtype=jnp.float32) * scale, 'W2': jax.random.normal(ks[3], (E, F, D), dtype=jnp.float32) * scale, 'W3': jax.random.normal(ks[4], (E, D, F), dtype=jnp.float32) * scale, 'b3': jax.random.normal(ks[5], (E, F), dtype=jnp.float32) * scale}
    _L0_ffn_all = _L0_ffn_setup()
    _L0_ffn_in = {k: v for k, v in _L0_ffn_all.items() if k in ('Wg', 'W1', 'W2', 'W3', 'b3')}
    del _L0_ffn_all
    return {'x': x, 'L0_conv_Wq': _L0_conv_in['Wq'], 'L0_conv_bq': _L0_conv_in['bq'], 'L0_conv_Wk': _L0_conv_in['Wk'], 'L0_conv_bk': _L0_conv_in['bk'], 'L0_conv_Wv': _L0_conv_in['Wv'], 'L0_conv_bv': _L0_conv_in['bv'], 'L0_conv_Wr': _L0_conv_in['Wr'], 'L0_conv_br': _L0_conv_in['br'], 'L0_ffn_Wg': _L0_ffn_in['Wg'], 'L0_ffn_W1': _L0_ffn_in['W1'], 'L0_ffn_W2': _L0_ffn_in['W2'], 'L0_ffn_W3': _L0_ffn_in['W3'], 'L0_ffn_b3': _L0_ffn_in['b3']}

def reference(x, L0_conv_Wq, L0_conv_bq, L0_conv_Wk, L0_conv_bk, L0_conv_Wv, L0_conv_bv, L0_conv_Wr, L0_conv_br, L0_ffn_Wg, L0_ffn_W1, L0_ffn_W2, L0_ffn_W3, L0_ffn_b3):
    import jax
    import jax.numpy as jnp

    def _L0_conv_ref(x, Wq, bq, Wk, bk, Wv, bv, Wr, br):
        import jax, jax.numpy as jnp
        import numpy as np
        B, H, W, C = (16, 16, 16, 128)
        DIM, VDIM = (64, 64)
        b, h, w, c = x.shape
        n = h * w
        q = (x @ Wq + bq).reshape(b, n, -1)
        k = (x @ Wk + bk).reshape(b, n, -1)
        v = (x @ Wv + bv).reshape(b, n, -1)
        attention_maps = jax.nn.softmax(k, axis=1)
        attention_vectors = jax.nn.softmax(v, axis=1)
        global_descriptors = jnp.einsum('bnd,bnv->bvd', q, attention_maps)
        out = jnp.einsum('bvd,bnv->bnd', global_descriptors, attention_vectors)
        out = out.reshape(b, h, w, -1)
        return out @ Wr + br

    def _L0_ffn_ref(x, Wg, W1, W2, W3, b3):
        import jax, jax.numpy as jnp
        import numpy as np
        NUM_EXPERTS = 8
        TOP_K = 2
        logits = jnp.einsum('bsd,de->bse', x, Wg)
        top_logits, top_idx = jax.lax.top_k(logits, TOP_K)
        top_w = jax.nn.softmax(top_logits, axis=-1)
        onehot = jax.nn.one_hot(top_idx, NUM_EXPERTS, dtype=x.dtype)
        C = jnp.sum(onehot * top_w[..., None], axis=-2)
        h = jnp.einsum('bsd,edf->bsef', x, W1)
        g = jnp.einsum('bsd,edf->bsef', x, W3) + b3
        act = jax.nn.silu(h) * g
        out = jnp.einsum('bse,bsef,efd->bsd', C, act, W2)
        return out

    def _gn(v, G=32, eps=1e-05):
        B_, H_, W_, C_ = v.shape
        g = v.reshape(B_, H_, W_, G, C_ // G)
        m = jnp.mean(g, axis=(1, 2, 4), keepdims=True)
        s = jnp.var(g, axis=(1, 2, 4), keepdims=True)
        return ((g - m) / jnp.sqrt(s + eps)).reshape(v.shape)

    def _ln_c(v, eps=1e-06):
        m = jnp.mean(v, axis=-1, keepdims=True)
        s = jnp.var(v, axis=-1, keepdims=True)
        return (v - m) / jnp.sqrt(s + eps)

    def _ln_t(v, eps=1e-05):
        m = jnp.mean(v, axis=-1, keepdims=True)
        s = jnp.var(v, axis=-1, keepdims=True)
        return (v - m) / jnp.sqrt(s + eps)

    def _to_tokens(v):
        B_, H_, W_, C_ = v.shape
        return v.reshape(B_, H_ * W_, C_)

    def _from_tokens(t, like):
        return t.reshape(like.shape)
    x = x + _L0_conv_ref(_ln_c(x), L0_conv_Wq, L0_conv_bq, L0_conv_Wk, L0_conv_bk, L0_conv_Wv, L0_conv_bv, L0_conv_Wr, L0_conv_br)
    t = _to_tokens(x)
    t = t + _L0_ffn_ref(_ln_t(t), L0_ffn_Wg, L0_ffn_W1, L0_ffn_W2, L0_ffn_W3, L0_ffn_b3)
    x = _from_tokens(t, x)
    return x

_drawn_inputs = setup_inputs


def setup_inputs(seed=0):
    import zlib

    import numpy as np

    out = dict(_drawn_inputs(seed))
    spreads = {'L0_conv_bq': (0.0, 0.8),
     'L0_conv_bk': (0.0, 0.8),
     'L0_conv_bv': (0.0, 0.8),
     'L0_conv_br': (0.0, 0.1)}
    factors = {'L0_conv_Wq': 8.0,
     'L0_conv_Wk': 8.0,
     'L0_conv_Wv': 8.0,
     'L0_conv_Wr': 8.0,
     'L0_ffn_Wg': 8.0,
     'L0_ffn_W1': 7.884,
     'L0_ffn_W2': 7.832,
     'L0_ffn_W3': 7.863,
     'L0_ffn_b3': 8.0}
    for name, (base, spread) in spreads.items():
        noise = np.random.default_rng([zlib.crc32(name.encode()), seed]).standard_normal(out[name].shape)
        drawn = base * np.exp(spread * noise) if base else spread * noise
        out[name] = jnp.asarray(drawn.astype(out[name].dtype))
    for name, factor in factors.items():
        out[name] = (out[name] * factor).astype(out[name].dtype)
    return out
```

```python
from contextlib import ExitStack

import concourse.bass as bass
from concourse import mybir

F32 = mybir.dt.float32
BF16 = mybir.dt.bfloat16
I32 = mybir.dt.int32
U32 = mybir.dt.uint32
ALU = mybir.AluOpType
ACT = mybir.ActivationFunctionType
AX = mybir.AxisListType

P = 128
LN_C_EPS = 1e-6
LN_T_EPS = 1e-5


def ds(start, size):
    return slice(start, start + size) if isinstance(start, int) else bass.ds(start, size)


class Step:

    def __init__(self, pair, offset):
        self.pair, self.offset = pair, offset
        self.par = offset % 2
        self.half = pair + offset // 2
        self.n = pair * 2 + offset

    def shift(self, k):
        return Step(self.pair, self.offset + k)


class Slot:

    def __init__(self, rnd, offset, ring, tiles):
        self.rnd, self.offset, self.size, self.tiles = rnd, offset, ring, tiles
        self.n = rnd * ring + offset
        self.par = offset % 2
        self.ring = offset % ring
        self.round = rnd + offset // ring

    def shift(self, k):
        return Slot(self.rnd, self.offset + k, self.size, self.tiles)

    def has(self, k):
        return not isinstance(self.n, int) or 0 <= self.n + k < self.tiles


def build(nc, x, Wq, bq, Wk, bk, Wv, bv, Wr, br, Wg, W1, W2, W3, b3, out):
    B, H, W, C = x.shape
    TOK = B * H * W
    NT = TOK // P
    DIM = Wq.shape[1]
    VDIM = Wk.shape[1]
    E, _, F = W1.shape
    TPU = 4
    NU = NT // TPU
    IMG = H * W
    K = 2
    KF = F // P
    REGION = TOK + P
    NS = (K * TOK + E * (P - 1)) // P
    SPARE = NS - K * TOK // P
    ROW = P + 2
    RING = 6
    DEST, WEIGHT = P, P + 1
    assert IMG == 2 * P and C == P and 2 * DIM == P and 2 * VDIM == P and NU % 2 == 0

    x_tok = x.rearrange("b h w c -> (b h w) c").rearrange("(b p s) c -> p b (s c)", p=P, s=2)
    out_tok = out.rearrange("b h w c -> (b h w) c").rearrange("(b p s) c -> p b (s c)", p=P, s=2)

    sorted_rows = nc.dram_tensor("sorted_rows", [E * REGION + SPARE * P, ROW], F32)
    result_rows = nc.dram_tensor("result_rows", [K * TOK + (E + SPARE) * P, P], F32)

    with ExitStack() as ctx:
        def sb(name, shape, dt=F32):
            return ctx.enter_context(nc.sbuf_tensor(name, shape, dt))

        def sem(name):
            return ctx.enter_context(nc.semaphore(name))

        bank = [ctx.enter_context(nc.psum_tensor(f"bank{i}", [P, 512], F32)) for i in range(8)]

        ident = sb("ident", [P, P])
        earlier = sb("earlier", [P, P], BF16)
        all_ones = sb("all_ones", [P, P], BF16)
        ones_row = sb("ones_row", [1, P])
        iota_e = sb("iota_e", [P, E])
        iota_ei = sb("iota_ei", [P, E], I32)
        region_i = sb("region_i", [P, E], I32)
        region = sb("region", [P, E])
        dest_ids = sb("dest_ids", [P, NT, K], I32)
        iota_s = sb("iota_s", [1, NS])
        iota_si = sb("iota_si", [1, NS], I32)
        eps_c = sb("eps_c", [P, 1])
        eps_t = sb("eps_t", [P, 1])
        pad_rows = sb("pad_rows", [P, E + SPARE, ROW])

        wvk = sb("wvk", [P, P])
        bvk = sb("bvk", [P, 1])
        wq = sb("wq", [P, DIM])
        bq_col = sb("bq_col", [DIM, 1])
        wr = sb("wr", [DIM, C])
        br_row = sb("br_row", [1, C])
        wq_t = sb("wq_t", [DIM, C])
        wqr = sb("wqr", [P, C])
        bqr_row = sb("bqr_row", [1, C])
        wg = sb("wg", [P, E])
        w1 = sb("w1", [P, E, F])
        w3 = sb("w3", [P, E, F])
        w2 = sb("w2", [P, E, KF, C])
        b3_all = sb("b3_all", [P, E, F])

        x_all = sb("x_all", [P, NT, C])
        x1_all = sb("x1_all", [P, NT, C])
        stats_c = sb("stats_c", [P, TPU, 6])
        mv_c = sb("mv_c", [P, TPU, 2])
        stats_t = sb("stats_t", [P, TPU, 6])
        mv_t = sb("mv_t", [P, TPU, 2])
        log_c = sb("log_c", [P, TPU])
        log_t = sb("log_t", [P, TPU])
        r0_c = sb("r0_c", [P, TPU])
        r0_t = sb("r0_t", [P, TPU])
        nt_c = [sb(f"newton_c{i}", [P, TPU]) for i in range(3)]
        nt_t = [sb(f"newton_t{i}", [P, TPU]) for i in range(3)]
        rstd_c = sb("rstd_c", [P, TPU])
        rstd_t = sb("rstd_t", [P, TPU])
        shift_c = sb("shift_c", [P, TPU])
        shift_t = sb("shift_t", [P, TPU])
        xn = [sb(f"xn{i}", [P, TPU, C]) for i in range(2)]
        xn_t = sb("xn_t", [P, TPU * P])
        col_max = sb("col_max", [P, 2])
        neg_max = sb("neg_max", [P, 2])
        exp_bias = sb("exp_bias", [P, 2])
        exps = sb("exps", [P, 2, IMG])
        exp_sum = sb("exp_sum", [P, 2])
        inv_sum = sb("inv_sum", [P, 2])
        probs = sb("probs", [P, 2, IMG])
        pk = sb("pk", [P, TPU, VDIM])
        xk = sb("xk", [P, 2 * VDIM])
        mix = sb("mix", [VDIM, 2 * C])
        row_buf = [sb(f"row_buf{i}", [P, TPU, K, ROW]) for i in range(2)]
        tn_t = sb("tn_t", [P, TPU * P])
        top = sb("top", [P, TPU, 8])
        top_idx = sb("top_idx", [P, TPU, 8], U32)
        chosen = sb("chosen", [P, K, TPU, E])
        member = sb("member", [P, TPU, E], BF16)
        member_sum = sb("member_sum", [P, E], BF16)
        seen = sb("seen", [P, E], BF16)
        gap = sb("gap", [P, TPU])
        gap_exp = sb("gap_exp", [P, TPU])
        gap_den = sb("gap_den", [P, TPU])
        place = sb("place", [P, TPU, E])
        place_of = sb("place_of", [P, K * TPU, E])
        position = [sb(f"position{i}", [P, K * TPU], I32) for i in range(2)]

        count_i = sb("count_i", [1, E], I32)
        count_up = sb("count_up", [1, E], I32)
        tiles_i = sb("tiles_i", [1, E], I32)
        tiles_f = sb("tiles_f", [1, E])
        ends = [sb(f"ends{i}", [1, E]) for i in range(4)]
        past = sb("past", [1, NS, E])
        past_tiles = sb("past_tiles", [1, NS, E])
        slot_e = sb("slot_e", [1, NS])
        slot_first = sb("slot_first", [1, NS])
        slot_in = sb("slot_in", [1, NS])
        slot_base = sb("slot_base", [1, NS])
        slot_row = sb("slot_row", [1, NS], I32)
        slot_expert = sb("slot_expert", [1, NS], I32)

        xs = [sb(f"xs{i}", [P, ROW]) for i in range(RING)]
        xs_t = [sb(f"xs_t{i}", [P, P]) for i in range(2)]
        silu_h = [sb(f"silu_h{i}", [P, F]) for i in range(2)]
        gate = [sb(f"gate{i}", [P, F]) for i in range(2)]
        act_rows = [sb(f"act_rows{i}", [P, F]) for i in range(2)]
        act_t = [sb(f"act_t{i}", [P, F]) for i in range(2)]
        ys = [sb(f"ys{i}", [P, P]) for i in range(RING)]

        y0 = [sb(f"y0_{i}", [P, TPU * C]) for i in range(2)]
        y1 = [sb(f"y1_{i}", [P, TPU * C]) for i in range(2)]
        half_sum = [sb(f"half_sum{i}", [P, TPU * C]) for i in range(2)]
        res = [sb(f"res{i}", [P, TPU * C]) for i in range(2)]

        pool_consts = sem("pool_consts")
        dve_consts = sem("dve_consts")
        small_in = sem("small_in")
        expert_in = sem("expert_in")
        wq_t_ps = sem("wq_t_ps")
        wq_t_sb = sem("wq_t_sb")
        wqr_ps = sem("wqr_ps")
        wqr_sb = sem("wqr_sb")
        x_in = [sem(f"x_in{i}") for i in range(2)]
        lnc_stats = sem("lnc_stats")
        lnc_r0 = sem("lnc_r0")
        lnc_rstd = sem("lnc_rstd")
        xn_ready = sem("xn_ready")
        xnt_ps = sem("xnt_ps")
        xnt_sb = sem("xnt_sb")
        kv_ps = sem("kv_ps")
        kv_bias = sem("kv_bias")
        exp_done = sem("exp_done")
        probs_ready = sem("probs_ready")
        pk_ps = sem("pk_ps")
        pk_sb = sem("pk_sb")
        xk_ps = sem("xk_ps")
        xk_sb = sem("xk_sb")
        mix_ps = sem("mix_ps")
        mix_sb = sem("mix_sb")
        attn_ps = sem("attn_ps")
        x1_ready = sem("x1_ready")
        lnt_stats = sem("lnt_stats")
        lnt_r0 = sem("lnt_r0")
        lnt_rstd = sem("lnt_rstd")
        tn_ready = sem("tn_ready")
        tnt_ps = sem("tnt_ps")
        tnt_sb = sem("tnt_sb")
        logits_ps = sem("logits_ps")
        member_ready = sem("member_ready")
        gap_ready = sem("gap_ready")
        gap_exp_ready = sem("gap_exp_ready")
        rank_ps = sem("rank_ps")
        rows_ready = sem("rows_ready")
        scattered = [sem(f"scattered{i}") for i in range(2)]
        bn_c_steps = sem("bn_c_steps")
        bn_t_steps = sem("bn_t_steps")
        newton_c_steps = sem("newton_c_steps")
        newton_t_steps = sem("newton_t_steps")
        max_steps = sem("max_steps")
        sum_steps = sem("sum_steps")
        pick_steps = sem("pick_steps")
        weight_steps = sem("weight_steps")
        place_steps = sem("place_steps")
        table_steps = sem("table_steps")
        log_c_steps = sem("log_c_steps")
        log_t_steps = sem("log_t_steps")
        pool_steps = sem("pool_steps")
        waited_dve = sem("waited_dve")
        waited_pool = sem("waited_pool")
        counts_ps = sem("counts_ps")
        count_ready = sem("count_ready")
        table_ready = sem("table_ready")
        pads_in = sem("pads_in")
        xs_in = [sem(f"xs_in{i}") for i in range(RING)]
        xst_ps = sem("xst_ps")
        xst_sb = sem("xst_sb")
        h_ps = sem("h_ps")
        g_ps = sem("g_ps")
        silu_ready = sem("silu_ready")
        gate_ready = sem("gate_ready")
        act_ready = sem("act_ready")
        actt_ps = sem("actt_ps")
        actt_sb = sem("actt_sb")
        y_ps = sem("y_ps")
        y_sb = sem("y_sb")
        y_out = [sem(f"y_out{i}") for i in range(RING)]
        y_in = [sem(f"y_in{i}") for i in range(2)]
        half_ready = sem("half_ready")
        res_ready = sem("res_ready")
        out_done = [sem(f"out_done{i}") for i in range(2)]

        POOL_CONSTS = 7
        SCATTERS = K * TPU
        block = ctx.enter_context(nc.Block())

        def at_least(eng, semaphore, value):
            if not (isinstance(value, int) and value <= 0):
                eng.wait_ge(semaphore, value)

        def wait_in_front(eng, own, *waits):
            for semaphore, value in waits:
                eng.wait_ge(semaphore, value)
            eng.sem_inc(own, 1)

        def run_slots(eng, step, before=None):
            if before is not None:
                before(Slot(0, 0, RING, NS))
            rounds = (NS - 1) // RING
            for o in range(RING):
                step(Slot(0, o, RING, NS))
            with eng.Fori(1, rounds) as q:
                for o in range(RING):
                    step(Slot(q, o, RING, NS))
            for n in range(rounds * RING, NS + 2):
                step(Slot(0, n, RING, NS))

        @block.sync
        def _(sp):
            def load_x(u):
                at_least(sp, x_in[u.par], u.half * 16)
                sp.dma_start(x_all[:, ds(u.n * TPU, TPU), :].rearrange("p (b s) c -> p b (s c)", s=2),
                             x_tok[:, ds(u.n * 2, 2), :]).then_inc(x_in[u.par], 16)

            load_x(Step(0, 0))
            load_x(Step(0, 1))
            with sp.Fori(1, NU // 2) as q:
                load_x(Step(q, 0))
                load_x(Step(q, 1))
            sp.dma_start(w1[:], W1.rearrange("e c f -> c e f")).then_inc(expert_in, 16)
            sp.dma_start(w3[:], W3.rearrange("e c f -> c e f")).then_inc(expert_in, 16)
            sp.dma_start(w2[:], W2.rearrange("e (k p) d -> p e k d", p=P)).then_inc(expert_in, 16)
            sp.dma_start(b3_all[:].rearrange("p e f -> p (e f)"),
                         b3.rearrange("e f -> (e f)").partition_broadcast(P)).then_inc(expert_in, 16)
            sp.wait_ge(pool_consts, POOL_CONSTS)
            for i in range(SPARE):
                first = E * REGION + i * P
                sp.dma_start(sorted_rows[first:first + P, :], pad_rows[:, E + i, :]).then_inc(pads_in, 16)
            sp.wait_ge(count_ready, 1)
            for e in range(E):
                n_rows = sp.value_load(count_i[0:1, e:e + 1], min_val=0, max_val=TOK)
                sp.dma_start(sorted_rows[ds(n_rows + e * REGION, P), :], pad_rows[:, e, :]).then_inc(pads_in, 16)
            sp.wait_ge(pads_in, 16 * (E + SPARE))
            for i in range(2):
                sp.wait_ge(scattered[i], 16 * SCATTERS * (NU // 2))
            sp.wait_ge(table_ready, 1)

            def load_rows(q, b):
                s = q * RING + b
                at_least(sp, y_out[b], q * 16)
                first = sp.value_load(slot_row[0:1, ds(s, 1)], min_val=0, max_val=E * REGION + (SPARE - 1) * P)
                sp.dma_start(xs[b][:], sorted_rows[ds(first, P), :]).then_inc(xs_in[b], 16)

            for b in range(RING):
                load_rows(0, b)
            with sp.Fori(1, NS // RING) as q:
                for b in range(RING):
                    load_rows(q, b)
            for b in range(NS % RING):
                load_rows(NS // RING, b)

            for b in range(RING):
                sp.wait_ge(y_out[b], 16 * ((NS - b + RING - 1) // RING))

            def load_results(u):
                at_least(sp, res_ready, u.n - 1)
                for k, y in ((0, y0), (1, y1)):
                    src = result_rows[ds(u.n * TPU * P + k * TOK, TPU * P), :]
                    sp.dma_start(y[u.par][:].rearrange("p (b m) -> p b m", b=2),
                                 src.rearrange("(b p s) c -> p b (s c)", p=P, s=2)).then_inc(y_in[u.par], 16)

            load_results(Step(0, 0))
            load_results(Step(0, 1))
            with sp.Fori(1, NU // 2) as q:
                load_results(Step(q, 0))
                load_results(Step(q, 1))

        @block.tensor
        def _(pe):
            def weights_product():
                nc.tensor.transpose(bank[4][0:DIM, 0:P], wq[:], ident[:]).then_inc(wq_t_ps, 1)
                pe.wait_ge(wq_t_sb, 1)
                nc.tensor.matmul(bank[5][:, 0:C], wq_t[:], wr[:], start=True, stop=True).then_inc(wqr_ps, 1)
                nc.tensor.matmul(bank[6][0:1, 0:C], bq_col[:], wr[:], start=True, stop=True).then_inc(wqr_ps, 1)

            def transpose_xn(u):
                pe.wait_ge(xn_ready, u.n + 1)
                at_least(pe, xnt_sb, u.n)
                for t in range(TPU):
                    last = nc.tensor.transpose(bank[0][:, t * P:(t + 1) * P], xn[u.par][:, t, :], ident[:])
                last.then_inc(xnt_ps, 1)

            def project_kv(u):
                pe.wait_ge(xnt_sb, u.n + 1)
                at_least(pe, exp_done, u.n)
                nc.tensor.matmul(bank[1][:], wvk[:], xn_t[:], start=True, stop=True).then_inc(kv_ps, 1)

            def transpose_probs(u):
                pe.wait_ge(probs_ready, u.n + 1)
                at_least(pe, pk_sb, u.n)
                for t in range(TPU):
                    last = nc.tensor.transpose(bank[2][:, t * P:(t + 1) * P],
                                               probs[:, t // 2, (t % 2) * P:(t % 2 + 1) * P], ident[:])
                last.then_inc(pk_ps, 1)

            def weigh_tokens(u):
                pe.wait_ge(pk_sb, u.n + 1)
                at_least(pe, mix_sb, u.n)
                for m in range(2):
                    for s in range(2):
                        last = nc.tensor.matmul(bank[3][:, m * VDIM:(m + 1) * VDIM], xn[u.par][:, 2 * m + s, :],
                                                pk[:, 2 * m + s, :], start=(s == 0), stop=(s == 1))
                last.then_inc(xk_ps, 1)

            def mix_channels(u):
                pe.wait_ge(xk_sb, u.n + 1)
                if isinstance(u.n, int) and u.n == 0:
                    pe.wait_ge(wqr_sb, 2)
                for m in range(2):
                    o = bank[3][0:VDIM, P + m * C:P + (m + 1) * C]
                    nc.tensor.matmul(o, xk[:, m * VDIM:(m + 1) * VDIM], wqr[:], start=True, stop=False)
                    last = nc.tensor.matmul(o, ones_row[:, 0:VDIM], bqr_row[:], start=False, stop=True)
                last.then_inc(mix_ps, 1)

            def attend(u):
                pe.wait_ge(mix_sb, u.n + 1)
                at_least(pe, x1_ready, u.n)
                for t in range(TPU):
                    m, s = t // 2, t % 2
                    o = bank[4][:, t * C:(t + 1) * C]
                    nc.tensor.matmul(o, probs[0:VDIM, m, s * P:(s + 1) * P], mix[:, m * C:(m + 1) * C],
                                     start=True, stop=False)
                    last = nc.tensor.matmul(o, ones_row[:], br_row[:], start=False, stop=True)
                last.then_inc(attn_ps, 1)

            def transpose_tn(u):
                pe.wait_ge(tn_ready, u.n + 1)
                at_least(pe, tnt_sb, u.n)
                for t in range(TPU):
                    last = nc.tensor.transpose(bank[5][:, t * P:(t + 1) * P], row_buf[u.par][:, t, 0, 0:C], ident[:])
                last.then_inc(tnt_ps, 1)

            def route(u):
                pe.wait_ge(tnt_sb, u.n + 1)
                at_least(pe, rows_ready, u.n)
                for t in range(TPU):
                    last = nc.tensor.matmul(bank[6][:, t * E:(t + 1) * E], tn_t[:, t * P:(t + 1) * P], wg[:],
                                            start=True, stop=True)
                last.then_inc(logits_ps, 1)

            def rank(u):
                pe.wait_ge(member_ready, u.n + 1)
                o = bank[7]
                nc.tensor.matmul(o[:, 0:TPU * E], earlier[:], member[:].rearrange("p t e -> p (t e)"),
                                 start=True, stop=False)
                nc.tensor.matmul(o[:, 0:TPU * E].rearrange("p (t e) -> p t e", e=E), all_ones[:],
                                 seen[:].unsqueeze(1).broadcast_to([P, TPU, E]), start=False, stop=False)
                for t in range(TPU - 1):
                    rest = TPU - 1 - t
                    last = nc.tensor.matmul(o[:, (t + 1) * E:TPU * E].rearrange("p (t e) -> p t e", e=E), all_ones[:],
                                            member[:, t:t + 1, :].broadcast_to([P, rest, E]),
                                            start=False, stop=(rest == 1))
                last.then_inc(rank_ps, 1)

            u = Step(0, 0)
            pe.wait_ge(pool_consts, POOL_CONSTS)
            transpose_xn(u)
            pe.wait_ge(small_in, 16 * 9)
            project_kv(u)
            weights_product()
            transpose_probs(u)
            weigh_tokens(u)
            mix_channels(u)
            attend(u)

            def both(u):
                old = u.shift(-1)
                transpose_xn(u)
                project_kv(u)
                transpose_tn(old)
                transpose_probs(u)
                route(old)
                weigh_tokens(u)
                mix_channels(u)
                attend(u)
                rank(old)

            with pe.Fori(0, NU // 2 - 1) as q:
                both(Step(q, 1))
                both(Step(q, 2))
            both(Step(0, NU - 1))
            u = Step(0, NU - 1)
            transpose_tn(u)
            route(u)
            rank(u)
            pe.wait_ge(rows_ready, NU)
            nc.tensor.matmul(bank[7][:, 0:E], all_ones[:], seen[:], start=True, stop=True).then_inc(counts_ps, 1)

            pe.wait_ge(table_ready, 1)
            pe.wait_ge(expert_in, 64)

            def transpose_rows(s, b):
                pe.wait_ge(xs_in[b], 16 * s.round + 16)
                at_least(pe, xst_sb, s.n)
                nc.tensor.transpose(bank[0][:, 0:P], xs[b][:, 0:P], ident[:]).then_inc(xst_ps, 1)

            def up(s):
                e = pe.value_load(slot_expert[0:1, ds(s.n, 1)], min_val=0, max_val=E - 1)
                pe.wait_ge(xst_sb, s.n + 1)
                at_least(pe, silu_ready, s.n - 1)
                w = w1[:, ds(e, 1), :].rearrange("p a f -> p (a f)")
                nc.tensor.matmul(bank[1 + s.par][:, 0:F], xs_t[s.par][:], w, start=True, stop=True).then_inc(h_ps, 1)
                at_least(pe, gate_ready, s.n - 1)
                w = w3[:, ds(e, 1), :].rearrange("p a f -> p (a f)")
                nc.tensor.matmul(bank[3 + s.par][:, 0:F], xs_t[s.par][:], w, start=True, stop=True).then_inc(g_ps, 1)

            def transpose_act(s):
                pe.wait_ge(act_ready, s.n + 1)
                at_least(pe, actt_sb, s.n - 1)
                for k in range(KF):
                    last = nc.tensor.transpose(bank[5 + s.par][:, k * P:(k + 1) * P],
                                               act_rows[s.par][:, k * P:(k + 1) * P], ident[:])
                last.then_inc(actt_ps, 1)

            def down(s):
                e = pe.value_load(slot_expert[0:1, ds(s.n, 1)], min_val=0, max_val=E - 1)
                pe.wait_ge(actt_sb, s.n + 1)
                at_least(pe, y_sb, s.n)
                for k in range(KF):
                    last = nc.tensor.matmul(bank[7][:, 0:C], act_t[s.par][:, k * P:(k + 1) * P],
                                            w2[:, ds(e, 1), k, :].rearrange("p a c -> p (a c)"),
                                            start=(k == 0), stop=(k == KF - 1))
                last.then_inc(y_ps, 1)

            def step(s):
                if s.has(1):
                    transpose_rows(s.shift(1), s.shift(1).ring)
                if s.has(0):
                    up(s)
                if s.has(-1):
                    transpose_act(s.shift(-1))
                if s.has(-2):
                    down(s.shift(-2))

            run_slots(pe, step, lambda s: transpose_rows(s, 0))

        @block.scalar
        def _(act):
            for dst, src in ((wvk[:, 0:VDIM], Wv), (wvk[:, VDIM:P], Wk), (wq[:], Wq), (wr[:], Wr), (wg[:], Wg),
                             (bvk[0:VDIM, :], bv.unsqueeze(1)), (bvk[VDIM:P, :], bk.unsqueeze(1)),
                             (bq_col[:], bq.unsqueeze(1)), (br_row[:], br.unsqueeze(0))):
                act.dma_start(dst, src).then_inc(small_in, 16)

            def seed_c(u):
                act.wait_ge(lnc_stats, u.n + 1)
                nc.scalar.activation(log_c[:], mv_c[:, :, 1], ACT.Ln, bias=eps_c[:, 0:1]).then_inc(log_c_steps, 1)
                act.wait_ge(log_c_steps, u.n + 1)
                nc.scalar.activation(r0_c[:], log_c[:], ACT.Exp, scale=-0.5).then_inc(lnc_r0, 1)

            def seed_t(u):
                act.wait_ge(lnt_stats, u.n + 1)
                nc.scalar.activation(log_t[:], mv_t[:, :, 1], ACT.Ln, bias=eps_t[:, 0:1]).then_inc(log_t_steps, 1)
                act.wait_ge(log_t_steps, u.n + 1)
                nc.scalar.activation(r0_t[:], log_t[:], ACT.Exp, scale=-0.5).then_inc(lnt_r0, 1)

            def copy_products():
                act.wait_ge(wq_t_ps, 1)
                nc.scalar.activation(wq_t[:], bank[4][0:DIM, 0:P], ACT.Copy).then_inc(wq_t_sb, 1)
                act.wait_ge(wqr_ps, 2)
                nc.scalar.activation(wqr[:], bank[5][:, 0:C], ACT.Copy).then_inc(wqr_sb, 1)
                nc.scalar.activation(bqr_row[:], bank[6][0:1, 0:C], ACT.Copy).then_inc(wqr_sb, 1)

            def normalise_x(u):
                act.wait_ge(lnc_rstd, u.n + 1)
                at_least(act, xk_ps, u.n - 1)
                for t in range(TPU):
                    last = nc.scalar.activation(xn[u.par][:, t, :],
                                                x_all[:, ds(u.n * TPU + t, 1), :].rearrange("p a c -> p (a c)"),
                                                ACT.Identity, bias=shift_c[:, t:t + 1], scale=rstd_c[:, t:t + 1])
                last.then_inc(xn_ready, 1)

            def copy_xnt(u):
                act.wait_ge(xnt_ps, u.n + 1)
                at_least(act, kv_ps, u.n)
                nc.scalar.activation(xn_t[:], bank[0][:], ACT.Copy).then_inc(xnt_sb, 1)

            def exp_kv(u):
                act.wait_ge(kv_bias, u.n + 1)
                at_least(act, probs_ready, u.n)
                for m in range(2):
                    last = nc.scalar.activation(exps[:, m, :], bank[1][:, m * IMG:(m + 1) * IMG], ACT.Exp,
                                                bias=exp_bias[:, m:m + 1], accum_out=exp_sum[:, m:m + 1])
                last.then_inc(exp_done, 1)

            def copy_pk(u):
                act.wait_ge(pk_ps, u.n + 1)
                at_least(act, xk_ps, u.n)
                nc.scalar.activation(pk[:], bank[2][:].rearrange("p (t v) -> p t v", t=TPU)[:, :, VDIM:P],
                                     ACT.Copy).then_inc(pk_sb, 1)

            def copy_xk(u):
                act.wait_ge(xk_ps, u.n + 1)
                at_least(act, mix_ps, u.n)
                nc.scalar.activation(xk[:], bank[3][:, 0:P], ACT.Copy).then_inc(xk_sb, 1)

            def copy_mix(u):
                act.wait_ge(mix_ps, u.n + 1)
                at_least(act, attn_ps, u.n)
                nc.scalar.activation(mix[:], bank[3][0:VDIM, P:P + 2 * C], ACT.Copy).then_inc(mix_sb, 1)

            def normalise_t(u):
                act.wait_ge(lnt_rstd, u.n + 1)
                at_least(act, scattered[u.par], u.half * (16 * SCATTERS))
                for t in range(TPU):
                    last = nc.scalar.activation(
                        row_buf[u.par][:, t, :, 0:C],
                        x1_all[:, ds(u.n * TPU + t, 1), :].broadcast_to([P, K, C]),
                        ACT.Identity, bias=shift_t[:, t:t + 1], scale=rstd_t[:, t:t + 1])
                last.then_inc(tn_ready, 1)

            def copy_tnt(u):
                act.wait_ge(tnt_ps, u.n + 1)
                at_least(act, logits_ps, u.n)
                nc.scalar.activation(tn_t[:], bank[5][:], ACT.Copy).then_inc(tnt_sb, 1)

            def exp_gap(u):
                act.wait_ge(gap_ready, u.n + 1)
                nc.scalar.activation(gap_exp[:], gap[:], ACT.Exp).then_inc(gap_exp_ready, 1)

            act.wait_ge(dve_consts, 1)
            u = Step(0, 0)
            seed_c(u)
            normalise_x(u)
            copy_xnt(u)
            exp_kv(u)
            copy_products()
            seed_c(u.shift(1))
            copy_pk(u)
            copy_xk(u)
            copy_mix(u)
            normalise_x(u.shift(1))

            def both(u, more=True):
                old, new = u.shift(-1), u.shift(1)
                copy_xnt(u)
                seed_t(old)
                exp_kv(u)
                normalise_t(old)
                if more:
                    seed_c(new)
                copy_pk(u)
                copy_tnt(old)
                copy_xk(u)
                copy_mix(u)
                exp_gap(old)
                if more:
                    normalise_x(new)

            with act.Fori(0, NU // 2 - 1) as q:
                both(Step(q, 1))
                both(Step(q, 2))
            both(Step(0, NU - 1), more=False)
            u = Step(0, NU - 1)
            seed_t(u)
            normalise_t(u)
            copy_tnt(u)
            exp_gap(u)

            def copy_rows_t(s):
                act.wait_ge(xst_ps, s.n + 1)
                at_least(act, g_ps, s.n - 1)
                nc.scalar.activation(xs_t[s.par][:], bank[0][:, 0:P], ACT.Copy).then_inc(xst_sb, 1)

            def silu(s):
                act.wait_ge(h_ps, s.n + 1)
                at_least(act, act_ready, s.n - 1)
                nc.scalar.activation(silu_h[s.par][:], bank[1 + s.par][:, 0:F], ACT.Silu).then_inc(silu_ready, 1)

            def copy_act_t(s):
                act.wait_ge(actt_ps, s.n + 1)
                at_least(act, y_ps, s.n - 1)
                nc.scalar.activation(act_t[s.par][:], bank[5 + s.par][:, 0:F], ACT.Copy).then_inc(actt_sb, 1)

            def scale_result(s):
                act.wait_ge(y_ps, s.n + 1)
                at_least(act, y_out[s.ring], s.round * 16)
                nc.scalar.activation(ys[s.ring][:], bank[7][:, 0:C], ACT.Copy,
                                     scale=xs[s.ring][:, WEIGHT:WEIGHT + 1]).then_inc(y_sb, 1)

            def step(s):
                if s.has(1):
                    copy_rows_t(s.shift(1))
                if s.has(-2):
                    copy_act_t(s.shift(-2))
                if s.has(0):
                    silu(s)
                if s.has(-2):
                    scale_result(s.shift(-2))

            run_slots(act, step, copy_rows_t)

            def store(u):
                act.wait_ge(res_ready, u.n + 1)
                act.dma_start(out_tok[:, ds(u.n * 2, 2), :],
                              res[u.par][:].rearrange("p (b m) -> p b m", b=2)).then_inc(out_done[u.par], 16)

            with act.Fori(0, NU // 2) as q:
                store(Step(q, 0))
                store(Step(q, 1))
            for i in range(2):
                act.wait_ge(out_done[i], 16 * (NU // 2))

        @block.vector
        def _(dve):
            nc.vector.memset(eps_c[:], LN_C_EPS)
            nc.vector.memset(eps_t[:], LN_T_EPS)
            nc.vector.memset(seen[:], 0.0)
            nc.vector.memset(ones_row[:], 1.0)
            nc.vector.memset(all_ones[:], 1.0).then_inc(dve_consts, 1)
            dve.wait_ge(pool_consts, POOL_CONSTS)
            nc.vector.tensor_copy(iota_e[:], iota_ei[:])
            nc.vector.tensor_copy(region[:], region_i[:])
            nc.vector.tensor_copy(iota_s[:], iota_si[:]).then_inc(dve_consts, 1)

            def after(ins, semaphore, value):
                ins.then_inc(semaphore, 1)
                dve.wait_ge(semaphore, value)

            def stats_of_x(u):
                wait_in_front(dve, waited_dve, (x_in[u.par], u.half * 16 + 16))
                for t in range(TPU):
                    last = nc.vector.bn_stats(stats_c[:, t, :],
                                              x_all[:, ds(u.n * TPU + t, 1), :].rearrange("p a c -> p (a c)"))
                last.then_inc(bn_c_steps, 1)
                wait_in_front(dve, waited_dve, (bn_c_steps, u.n + 1))
                for t in range(TPU):
                    last = nc.vector.bn_aggr(mv_c[:, t, :], stats_c[:, t, :])
                last.then_inc(lnc_stats, 1)

            def stats_of_x1(u):
                wait_in_front(dve, waited_dve, (x1_ready, u.n + 1))
                for t in range(TPU):
                    last = nc.vector.bn_stats(stats_t[:, t, :],
                                              x1_all[:, ds(u.n * TPU + t, 1), :].rearrange("p a c -> p (a c)"))
                last.then_inc(bn_t_steps, 1)
                wait_in_front(dve, waited_dve, (bn_t_steps, u.n + 1))
                for t in range(TPU):
                    last = nc.vector.bn_aggr(mv_t[:, t, :], stats_t[:, t, :])
                last.then_inc(lnt_stats, 1)

            def newton(u, mv, eps, r0, tmp, rstd, shift, own, done):
                after(nc.vector.tensor_tensor(tmp[0][:], r0[:], r0[:], ALU.mult), own, u.n * 4 + 1)
                after(nc.vector.scalar_tensor_tensor(out=tmp[1][:], in0=mv[:, :, 1], scalar=eps, in1=tmp[0][:],
                                                     op0=ALU.add, op1=ALU.mult), own, u.n * 4 + 2)
                after(nc.vector.tensor_scalar(tmp[2][:], tmp[1][:], -0.5, 1.5, ALU.mult, ALU.add), own, u.n * 4 + 3)
                after(nc.vector.tensor_tensor(rstd[:], r0[:], tmp[2][:], ALU.mult), own, u.n * 4 + 4)
                nc.vector.scalar_tensor_tensor(out=shift[:], in0=mv[:, :, 0], scalar=-1.0, in1=rstd[:],
                                               op0=ALU.mult, op1=ALU.mult).then_inc(done, 1)

            def rstd_of_x(u):
                dve.wait_ge(lnc_r0, u.n + 1)
                at_least(dve, xn_ready, u.n)
                newton(u, mv_c, LN_C_EPS, r0_c, nt_c, rstd_c, shift_c, newton_c_steps, lnc_rstd)

            def rstd_of_x1(u):
                dve.wait_ge(lnt_r0, u.n + 1)
                at_least(dve, tn_ready, u.n)
                newton(u, mv_t, LN_T_EPS, r0_t, nt_t, rstd_t, shift_t, newton_t_steps, lnt_rstd)

            def max_kv(u):
                dve.wait_ge(kv_ps, u.n + 1)
                after(nc.vector.tensor_reduce(col_max[:], bank[1][:].rearrange("p (m n) -> p m n", m=2), AX.X,
                                              ALU.max), max_steps, u.n * 2 + 1)
                after(nc.vector.tensor_scalar(neg_max[:], col_max[:], bvk[:, 0:1], -1.0, ALU.add, ALU.mult),
                      max_steps, u.n * 2 + 2)
                nc.vector.tensor_scalar(exp_bias[:], neg_max[:], bvk[:, 0:1], None, ALU.add).then_inc(kv_bias, 1)

            def normalise_probs(u):
                dve.wait_ge(exp_done, u.n + 1)
                after(nc.vector.reciprocal(inv_sum[:], exp_sum[:]), sum_steps, u.n + 1)
                at_least(dve, attn_ps, u.n)
                for m in range(2):
                    last = nc.vector.tensor_scalar(probs[:, m, :], exps[:, m, :], inv_sum[:, m:m + 1], None, ALU.mult)
                last.then_inc(probs_ready, 1)

            def add_x(u):
                dve.wait_ge(attn_ps, u.n + 1)
                nc.vector.tensor_tensor(x1_all[:, ds(u.n * TPU, TPU), :],
                                        bank[4][:].rearrange("p (t c) -> p t c", t=TPU),
                                        x_all[:, ds(u.n * TPU, TPU), :], ALU.add).then_inc(x1_ready, 1)

            def choose(u):
                wait_in_front(dve, waited_dve, (logits_ps, u.n + 1))
                for t in range(TPU):
                    last = nc.vector.max(top[:, t, :], bank[6][:, t * E:(t + 1) * E])
                after(last, pick_steps, u.n * 3 + 1)
                nc.vector.tensor_tensor(gap[:], top[:, :, 1], top[:, :, 0], ALU.subtract).then_inc(gap_ready, 1)
                for t in range(TPU):
                    last = nc.vector.max_index(top_idx[:, t, :], top[:, t, :], bank[6][:, t * E:(t + 1) * E])
                after(last, pick_steps, u.n * 3 + 2)
                after(nc.vector.tensor_tensor(
                    chosen[:], iota_e[:].unsqueeze(1).unsqueeze(1).broadcast_to([P, K, TPU, E]),
                    top_idx[:, :, 0:K].rearrange("p t k -> p k t").unsqueeze(3).broadcast_to([P, K, TPU, E]),
                    ALU.is_equal), pick_steps, u.n * 3 + 3)
                nc.vector.tensor_tensor(member[:], chosen[:, 0], chosen[:, 1], ALU.add).then_inc(member_ready, 1)

            def weigh_and_place(u):
                rows_i = row_buf[u.par][:].bitcast(I32)
                at_least(dve, scattered[u.par], u.half * (16 * SCATTERS))
                nc.vector.tensor_copy(rows_i[:, :, :, DEST], dest_ids[:, ds(u.n * TPU, TPU), :])
                dve.wait_ge(gap_exp_ready, u.n + 1)
                after(nc.vector.tensor_scalar(gap_den[:], gap_exp[:], 1.0, None, ALU.add), weight_steps, u.n * 2 + 1)
                after(nc.vector.reciprocal(row_buf[u.par][:, :, 0, WEIGHT], gap_den[:]), weight_steps, u.n * 2 + 2)
                nc.vector.tensor_tensor(row_buf[u.par][:, :, 1, WEIGHT], gap_exp[:], row_buf[u.par][:, :, 0, WEIGHT],
                                        ALU.mult)
                dve.wait_ge(rank_ps, u.n + 1)
                after(nc.vector.tensor_tensor(place[:], bank[7][:, 0:TPU * E].rearrange("p (t e) -> p t e", e=E),
                                              region[:].unsqueeze(1).broadcast_to([P, TPU, E]), ALU.add),
                      place_steps, u.n * 3 + 1)
                after(nc.vector.tensor_tensor(place_of[:].rearrange("p (k t) e -> p k t e", k=K), chosen[:],
                                              place[:].unsqueeze(1).broadcast_to([P, K, TPU, E]), ALU.mult),
                      place_steps, u.n * 3 + 2)
                with nc.allow_low_precision("whole numbers below 2^24, and sums of up to four ones"):
                    nc.vector.tensor_reduce(position[u.par][:], place_of[:], AX.X, ALU.add)
                    after(nc.vector.tensor_reduce(member_sum[:], member[:].rearrange("p t e -> p e t"), AX.X, ALU.add),
                          place_steps, u.n * 3 + 3)
                nc.vector.tensor_tensor(seen[:], seen[:], member_sum[:], ALU.add).then_inc(rows_ready, 1)

            u = Step(0, 0)
            stats_of_x(u)
            rstd_of_x(u)
            dve.wait_ge(small_in, 16 * 9)
            max_kv(u)
            stats_of_x(u.shift(1))
            normalise_probs(u)
            rstd_of_x(u.shift(1))
            add_x(u)

            def both(u, more=True):
                old, new = u.shift(-1), u.shift(1)
                stats_of_x1(old)
                max_kv(u)
                rstd_of_x1(old)
                if more:
                    stats_of_x(new)
                normalise_probs(u)
                if more:
                    rstd_of_x(new)
                choose(old)
                add_x(u)
                weigh_and_place(old)

            with dve.Fori(0, NU // 2 - 1) as q:
                both(Step(q, 1))
                both(Step(q, 2))
            both(Step(0, NU - 1), more=False)
            u = Step(0, NU - 1)
            stats_of_x1(u)
            rstd_of_x1(u)
            choose(u)
            weigh_and_place(u)

            chain = [0]

            def link(ins):
                chain[0] += 1
                after(ins, table_steps, chain[0])

            dve.wait_ge(counts_ps, 1)
            nc.vector.tensor_copy(count_i[:], bank[7][0:1, 0:E]).then_inc(count_ready, 1)
            link(nc.vector.tensor_scalar(count_up[:], bank[7][0:1, 0:E], float(P - 1), None, ALU.add))
            link(nc.vector.tensor_single_scalar(tiles_i[:], count_up[:], P.bit_length() - 1, ALU.arith_shift_right))
            link(nc.vector.tensor_copy(tiles_f[:], tiles_i[:]))
            run = tiles_f
            for i in range(E.bit_length() - 1):
                d = 1 << i
                nc.vector.tensor_copy(ends[i][:, 0:d], run[:, 0:d])
                link(nc.vector.tensor_tensor(ends[i][:, d:E], run[:, d:E], run[:, 0:E - d], ALU.add))
                run = ends[i]
            link(nc.vector.tensor_tensor(past[:], run[:].unsqueeze(1).broadcast_to([1, NS, E]),
                                         iota_s[:].unsqueeze(2).broadcast_to([1, NS, E]), ALU.is_le))
            nc.vector.tensor_reduce(slot_e[:], past[:], AX.X, ALU.add)
            link(nc.vector.tensor_tensor(past_tiles[:], past[:], tiles_f[:].unsqueeze(1).broadcast_to([1, NS, E]),
                                         ALU.mult))
            nc.vector.tensor_scalar(slot_expert[:], slot_e[:], float(E - 1), None, ALU.min)
            link(nc.vector.tensor_reduce(slot_first[:], past_tiles[:], AX.X, ALU.add))
            link(nc.vector.tensor_tensor(slot_in[:], iota_s[:], slot_first[:], ALU.subtract))
            link(nc.vector.tensor_scalar(slot_base[:], slot_e[:], float(REGION), None, ALU.mult))
            nc.vector.scalar_tensor_tensor(out=slot_row[:], in0=slot_in[:], scalar=float(P), in1=slot_base[:],
                                           op0=ALU.mult, op1=ALU.add).then_inc(table_ready, 1)
            dve.wait_ge(table_ready, 1)
            dve.wait_ge(expert_in, 64)

            def gated(s):
                e = dve.value_load(slot_expert[0:1, ds(s.n, 1)], min_val=0, max_val=E - 1)
                dve.wait_ge(g_ps, s.n + 1)
                nc.vector.tensor_tensor(gate[s.par][:], bank[3 + s.par][:, 0:F],
                                        b3_all[:, ds(e, 1), :].rearrange("p a f -> p (a f)"),
                                        ALU.add).then_inc(gate_ready, 1)
                dve.wait_ge(gate_ready, s.n + 1)
                dve.wait_ge(silu_ready, s.n + 1)
                at_least(dve, actt_ps, s.n - 1)
                nc.vector.tensor_tensor(act_rows[s.par][:], silu_h[s.par][:], gate[s.par][:],
                                        ALU.mult).then_inc(act_ready, 1)

            def step(s):
                if s.has(0):
                    gated(s)

            run_slots(dve, step)

            def combine(u):
                dve.wait_ge(y_in[u.par], u.half * 32 + 32)
                nc.vector.tensor_tensor(half_sum[u.par][:], y0[u.par][:], y1[u.par][:], ALU.add).then_inc(half_ready, 1)
                dve.wait_ge(half_ready, u.n + 1)
                at_least(dve, out_done[u.par], u.half * 16)
                nc.vector.tensor_tensor(res[u.par][:], half_sum[u.par][:],
                                        x1_all[:, ds(u.n * TPU, TPU), :].rearrange("p t c -> p (t c)"),
                                        ALU.add).then_inc(res_ready, 1)

            combine(Step(0, 0))
            combine(Step(0, 1))
            with dve.Fori(1, NU // 2) as q:
                combine(Step(q, 0))
                combine(Step(q, 1))

        @block.gpsimd
        def _(pool):
            nc.gpsimd.memset(ident[:], 0.0)
            nc.gpsimd.memset(earlier[:], 1.0)
            nc.gpsimd.memset(pad_rows[:], 0.0).then_inc(pool_steps, 1)
            pool.wait_ge(pool_steps, 1)
            nc.gpsimd.affine_select(out=ident[:], in_=ident[:], compare_op=ALU.not_equal, fill=1.0, base=0,
                                    pattern=[[-1, P]], channel_multiplier=1).then_inc(pool_consts, 1)
            nc.gpsimd.affine_select(out=earlier[:], in_=earlier[:], compare_op=ALU.is_gt, fill=0.0, base=0,
                                    pattern=[[1, P]], channel_multiplier=-1).then_inc(pool_consts, 1)
            nc.gpsimd.iota(iota_ei[:], [[1, E]], base=0, channel_multiplier=0).then_inc(pool_consts, 1)
            nc.gpsimd.iota(region_i[:], [[REGION, E]], base=0, channel_multiplier=0).then_inc(pool_consts, 1)
            nc.gpsimd.iota(dest_ids[:].rearrange("p (b s) k -> p b s k", s=2), [[2 * P, NT // 2], [1, 2], [TOK, K]],
                           base=0, channel_multiplier=2).then_inc(pool_consts, 1)
            nc.gpsimd.iota(iota_si[:], [[1, NS]], base=0, channel_multiplier=0).then_inc(pool_consts, 1)
            nc.gpsimd.iota(pad_rows[:].bitcast(I32)[:, :, DEST], [[P, E + SPARE]], base=K * TOK,
                           channel_multiplier=1).then_inc(pool_consts, 1)

            def scatter_rows(u):
                wait_in_front(pool, waited_pool, (tn_ready, u.n + 1), (rows_ready, u.n + 1))
                for k in range(K):
                    for t in range(TPU):
                        c = k * TPU + t
                        nc.gpsimd.indirect_dma_start(
                            out=sorted_rows.ap(),
                            out_offset=bass.IndirectOffsetOnAxis(ap=position[u.par][:, c:c + 1], axis=0),
                            in_=row_buf[u.par][:, t, k, :], in_offset=None).then_inc(scattered[u.par], 16)

            with pool.Fori(0, NU // 2) as q:
                scatter_rows(Step(q, 0))
                scatter_rows(Step(q, 1))

            def scatter_results(s):
                wait_in_front(pool, waited_pool, (y_sb, s.n + 1))
                nc.gpsimd.indirect_dma_start(
                    out=result_rows.ap(),
                    out_offset=bass.IndirectOffsetOnAxis(ap=xs[s.ring][:].bitcast(I32)[:, DEST:DEST + 1], axis=0),
                    in_=ys[s.ring][:], in_offset=None).then_inc(y_out[s.ring], 16)

            with pool.Fori(0, NS // RING) as q:
                for o in range(RING):
                    scatter_results(Slot(q, o, RING, NS))
            for n in range(NS // RING * RING, NS):
                scatter_results(Slot(0, n, RING, NS))


INPUTS = ("x", "L0_conv_Wq", "L0_conv_bq", "L0_conv_Wk", "L0_conv_bk", "L0_conv_Wv", "L0_conv_bv", "L0_conv_Wr",
          "L0_conv_br", "L0_ffn_Wg", "L0_ffn_W1", "L0_ffn_W2", "L0_ffn_W3", "L0_ffn_b3")


def kernel(**inputs):
    import numpy as np
    import concourse.bacc as bacc
    from concourse.bass_utils import run_bass_kernel_spmd

    nc = bacc.Bacc("TRN2", target_bir_lowering=False, num_devices=1)
    arrays, args = {}, []
    for name in INPUTS:
        a = np.ascontiguousarray(inputs[name])
        arrays[f"{name}_dram"] = a
        args.append(nc.dram_tensor(f"{name}_dram", a.shape, mybir.dt.from_np(a.dtype), kind="ExternalInput").ap())
    out = nc.dram_tensor("out_dram", inputs["x"].shape, F32, kind="ExternalOutput").ap()
    build(nc, *args, out)
    got = run_bass_kernel_spmd(nc, [arrays], core_ids=[0])
    return got.results[0]["out_dram"]
```

```python
from contextlib import ExitStack

import concourse.bass as bass
from concourse import mybir

F32 = mybir.dt.float32
BF16 = mybir.dt.bfloat16
I32 = mybir.dt.int32
U32 = mybir.dt.uint32
ALU = mybir.AluOpType
ACT = mybir.ActivationFunctionType
AX = mybir.AxisListType

P = 128
LN_C_EPS = 1e-6
LN_T_EPS = 1e-5


def ds(start, size):
    return slice(start, start + size) if isinstance(start, int) else bass.ds(start, size)


class Step:

    def __init__(self, pair, offset):
        self.pair, self.offset = pair, offset
        self.par = offset % 2
        self.half = pair + offset // 2
        self.n = pair * 2 + offset

    def shift(self, k):
        return Step(self.pair, self.offset + k)


class Slot:

    def __init__(self, rnd, offset, ring, tiles):
        self.rnd, self.offset, self.size, self.tiles = rnd, offset, ring, tiles
        self.n = rnd * ring + offset
        self.par = offset % 2
        self.ring = offset % ring
        self.round = rnd + offset // ring

    def shift(self, k):
        return Slot(self.rnd, self.offset + k, self.size, self.tiles)

    def has(self, k):
        return not isinstance(self.n, int) or 0 <= self.n + k < self.tiles


def build(nc, x, Wq, bq, Wk, bk, Wv, bv, Wr, br, Wg, W1, W2, W3, b3, out):
    B, H, W, C = x.shape
    TOK = B * H * W
    NT = TOK // P
    DIM = Wq.shape[1]
    VDIM = Wk.shape[1]
    E, _, F = W1.shape
    TPU = 4
    NU = NT // TPU
    IMG = H * W
    K = 2
    KF = F // P
    REGION = TOK + P
    NS = (K * TOK + E * (P - 1)) // P
    SPARE = NS - K * TOK // P
    ROW = P + 2
    RING = 10
    DEST, WEIGHT = P, P + 1
    assert IMG == 2 * P and C == P and 2 * DIM == P and 2 * VDIM == P and NU % 2 == 0

    x_tok = x.rearrange("b h w c -> (b h w) c").rearrange("(b p s) c -> p b (s c)", p=P, s=2)
    out_tok = out.rearrange("b h w c -> (b h w) c").rearrange("(b p s) c -> p b (s c)", p=P, s=2)

    sorted_rows = nc.dram_tensor("sorted_rows", [E * REGION + SPARE * P, ROW], F32)
    result_rows = nc.dram_tensor("result_rows", [K * TOK + (E + SPARE) * P, P], F32)

    with ExitStack() as ctx:
        def sb(name, shape, dt=F32):
            return ctx.enter_context(nc.sbuf_tensor(name, shape, dt))

        def sem(name):
            return ctx.enter_context(nc.semaphore(name))

        bank = [ctx.enter_context(nc.psum_tensor(f"bank{i}", [P, 512], F32)) for i in range(8)]

        ident = sb("ident", [P, P])
        earlier = sb("earlier", [P, P], BF16)
        all_ones = sb("all_ones", [P, P], BF16)
        iota_e = sb("iota_e", [P, E])
        iota_ei = sb("iota_ei", [P, E], I32)
        region_i = sb("region_i", [P, E], I32)
        region = sb("region", [P, E])
        dest_ids = sb("dest_ids", [P, NT, K], I32)
        iota_s = sb("iota_s", [1, NS])
        iota_si = sb("iota_si", [1, NS], I32)
        eps = sb("eps", [P, 2, TPU])
        pad_rows = sb("pad_rows", [P, E + SPARE, ROW])

        wkv = sb("wkv", [P, P])
        bkv = sb("bkv", [P, 1])
        wq = sb("wq", [P, DIM])
        bq_col = sb("bq_col", [DIM, 1])
        wr = sb("wr", [DIM, C])
        br_all = sb("br_all", [P, C])
        wq_t = sb("wq_t", [DIM, C])
        wqr = sb("wqr", [P, C])
        bq_wide = sb("bq_wide", [DIM, P])
        bqr = sb("bqr", [P, C])
        wg = sb("wg", [P, E])
        w1 = sb("w1", [P, E, F])
        w3 = sb("w3", [P, E, F])
        w2 = sb("w2", [P, E, KF, C])
        b3_all = sb("b3_all", [P, E, F])

        x_all = sb("x_all", [P, NT, C])
        x1_all = sb("x1_all", [P, NT, C])
        stats = sb("stats", [P, 2, TPU, 6])
        mean_var = sb("mean_var", [P, 2, TPU, 2])
        var_eps = sb("var_eps", [P, 2, TPU])
        power = sb("power", [P, 2, TPU])
        rstd = sb("rstd", [P, 2, TPU])
        shift = sb("shift", [P, 2, TPU])
        xn = [sb(f"xn{i}", [P, TPU, C]) for i in range(2)]
        xn_t = sb("xn_t", [P, TPU * P])
        col_max = sb("col_max", [P, 2])
        neg_max = sb("neg_max", [P, 2])
        exp_bias = sb("exp_bias", [P, 2])
        exps = sb("exps", [P, 2, IMG])
        exp_sum = sb("exp_sum", [P, 2])
        inv_sum = sb("inv_sum", [P, 2])
        probs = [sb(f"probs{i}", [P, 2, IMG]) for i in range(2)]
        pk = sb("pk", [P, TPU, VDIM])
        xk = sb("xk", [P, 2 * VDIM])
        mix = sb("mix", [P, 2 * C])
        row_buf = [sb(f"row_buf{i}", [P, TPU, K, ROW]) for i in range(2)]
        tn_t = sb("tn_t", [P, TPU * P])
        top = sb("top", [P, TPU, 8])
        top_idx = sb("top_idx", [P, TPU, 8], U32)
        chosen = sb("chosen", [P, K, TPU, E])
        member = sb("member", [P, TPU, E], BF16)
        member_sum = sb("member_sum", [P, E], BF16)
        seen = sb("seen", [P, E], BF16)
        gap = sb("gap", [P, TPU])
        gap_exp = sb("gap_exp", [P, TPU])
        gap_den = sb("gap_den", [P, TPU])
        place = sb("place", [P, TPU, E])
        place_of = sb("place_of", [P, K * TPU, E])
        position = [sb(f"position{i}", [P, K * TPU], I32) for i in range(2)]

        count_i = sb("count_i", [1, E], I32)
        count_up = sb("count_up", [1, E], I32)
        tiles_i = sb("tiles_i", [1, E], I32)
        tiles_f = sb("tiles_f", [1, E])
        ends = [sb(f"ends{i}", [1, E]) for i in range(4)]
        past = sb("past", [1, NS, E])
        past_tiles = sb("past_tiles", [1, NS, E])
        slot_e = sb("slot_e", [1, NS])
        slot_first = sb("slot_first", [1, NS])
        slot_in = sb("slot_in", [1, NS])
        slot_base = sb("slot_base", [1, NS])
        slot_row = sb("slot_row", [1, NS], I32)
        slot_expert = sb("slot_expert", [1, NS], I32)

        xs = [sb(f"xs{i}", [P, ROW]) for i in range(RING)]
        xs_t = [sb(f"xs_t{i}", [P, P]) for i in range(2)]
        silu_h = [sb(f"silu_h{i}", [P, F]) for i in range(2)]
        gate = [sb(f"gate{i}", [P, F]) for i in range(2)]
        act_rows = [sb(f"act_rows{i}", [P, F]) for i in range(2)]
        act_t = [sb(f"act_t{i}", [P, F]) for i in range(2)]
        ys = [sb(f"ys{i}", [P, P]) for i in range(RING)]

        y0 = [sb(f"y0_{i}", [P, TPU * C]) for i in range(2)]
        y1 = [sb(f"y1_{i}", [P, TPU * C]) for i in range(2)]
        half_sum = [sb(f"half_sum{i}", [P, TPU * C]) for i in range(2)]
        res = [sb(f"res{i}", [P, TPU * C]) for i in range(2)]

        pool_consts = sem("pool_consts")
        dve_consts = sem("dve_consts")
        small_in = sem("small_in")
        expert_in = sem("expert_in")
        wq_t_ps = sem("wq_t_ps")
        wq_t_sb = sem("wq_t_sb")
        wqr_ps = sem("wqr_ps")
        wqr_sb = sem("wqr_sb")
        x_in = [sem(f"x_in{i}") for i in range(2)]
        rstd_ready = sem("rstd_ready")
        shift_ready = sem("shift_ready")
        x_br_ready = sem("x_br_ready")
        xn_ready = sem("xn_ready")
        xnt_ps = sem("xnt_ps")
        xnt_sb = sem("xnt_sb")
        kv_ps = sem("kv_ps")
        kv_bias = sem("kv_bias")
        exp_done = sem("exp_done")
        probs_ready = sem("probs_ready")
        pk_ps = sem("pk_ps")
        pk_sb = sem("pk_sb")
        xk_ps = sem("xk_ps")
        xk_sb = sem("xk_sb")
        mix_ps = sem("mix_ps")
        mix_sb = sem("mix_sb")
        attn_ps = sem("attn_ps")
        x1_ready = sem("x1_ready")
        tn_ready = sem("tn_ready")
        tnt_ps = sem("tnt_ps")
        tnt_sb = sem("tnt_sb")
        logits_ps = sem("logits_ps")
        member_ready = sem("member_ready")
        gap_ready = sem("gap_ready")
        gap_exp_ready = sem("gap_exp_ready")
        rank_ps = sem("rank_ps")
        rows_ready = sem("rows_ready")
        rows_free = sem("rows_free")
        scattered = [sem(f"scattered{i}") for i in range(2)]
        bn_c_steps = sem("bn_c_steps")
        bn_t_steps = sem("bn_t_steps")
        power_steps = sem("power_steps")
        bq_wide_ready = sem("bq_wide_ready")
        max_steps = sem("max_steps")
        sum_steps = sem("sum_steps")
        pick_steps = sem("pick_steps")
        weight_steps = sem("weight_steps")
        place_steps = sem("place_steps")
        table_steps = sem("table_steps")
        pool_steps = sem("pool_steps")
        waited_dve = sem("waited_dve")
        waited_pool = sem("waited_pool")
        waited_pe = sem("waited_pe")
        counts_ps = sem("counts_ps")
        count_ready = sem("count_ready")
        table_ready = sem("table_ready")
        pads_in = sem("pads_in")
        xs_in = [sem(f"xs_in{i}") for i in range(RING)]
        xst_ps = sem("xst_ps")
        xst_sb = sem("xst_sb")
        h_ps = sem("h_ps")
        g_ps = sem("g_ps")
        silu_ready = sem("silu_ready")
        gate_ready = sem("gate_ready")
        act_ready = sem("act_ready")
        actt_ps = sem("actt_ps")
        actt_sb = sem("actt_sb")
        y_ps = sem("y_ps")
        y_sb = sem("y_sb")
        y_out = [sem(f"y_out{i}") for i in range(RING)]
        y_in = [sem(f"y_in{i}") for i in range(2)]
        half_ready = sem("half_ready")
        res_ready = sem("res_ready")
        out_done = [sem(f"out_done{i}") for i in range(2)]

        POOL_CONSTS = 7
        SCATTERS = K * TPU
        block = ctx.enter_context(nc.Block())

        def at_least(eng, semaphore, value):
            if not (isinstance(value, int) and value <= 0):
                eng.wait_ge(semaphore, value)

        def wait_in_front(eng, own, *waits):
            for semaphore, value in waits:
                eng.wait_ge(semaphore, value)
            eng.sem_inc(own, 1)

        class units:

            @staticmethod
            def has(u):
                return not isinstance(u.n, int) or 0 <= u.n < NU

            @staticmethod
            def upto(n):
                return min(n, NU) if isinstance(n, int) else n

            @staticmethod
            def read(n):
                return [] if isinstance(n, int) and n <= 0 else [(rstd_ready, n), (shift_ready, n)]

        def run_units(eng, iteration):
            for i in range(-1, 2):
                iteration(Step(0, i))
            with eng.Fori(1, NU // 2 - 1) as q:
                iteration(Step(q, 0))
                iteration(Step(q, 1))
            for i in range(NU - 2, NU + 1):
                iteration(Step(0, i))

        def run_slots(eng, step, before=None):
            if before is not None:
                before(Slot(0, 0, RING, NS))
            rounds = (NS - 1) // RING
            for o in range(RING):
                step(Slot(0, o, RING, NS))
            with eng.Fori(1, rounds) as q:
                for o in range(RING):
                    step(Slot(q, o, RING, NS))
            for n in range(rounds * RING, NS + 2):
                step(Slot(0, n, RING, NS))

        @block.sync
        def _(sp):
            def load_x(u):
                at_least(sp, x_in[u.par], u.half * 16)
                sp.dma_start(x_all[:, ds(u.n * TPU, TPU), :].rearrange("p (b s) c -> p b (s c)", s=2),
                             x_tok[:, ds(u.n * 2, 2), :]).then_inc(x_in[u.par], 16)

            load_x(Step(0, 0))
            load_x(Step(0, 1))
            with sp.Fori(1, NU // 2) as q:
                load_x(Step(q, 0))
                load_x(Step(q, 1))
            sp.dma_start(w1[:], W1.rearrange("e c f -> c e f")).then_inc(expert_in, 16)
            sp.dma_start(w3[:], W3.rearrange("e c f -> c e f")).then_inc(expert_in, 16)
            sp.dma_start(w2[:], W2.rearrange("e (k p) d -> p e k d", p=P)).then_inc(expert_in, 16)
            sp.dma_start(b3_all[:].rearrange("p e f -> p (e f)"),
                         b3.rearrange("e f -> (e f)").partition_broadcast(P)).then_inc(expert_in, 16)
            sp.wait_ge(pool_consts, POOL_CONSTS)
            for i in range(SPARE):
                first = E * REGION + i * P
                sp.dma_start(sorted_rows[first:first + P, :], pad_rows[:, E + i, :]).then_inc(pads_in, 16)

            def free_rows(u):
                sp.wait_ge(scattered[u.par], u.half * (16 * SCATTERS) + 16 * SCATTERS)
                sp.sem_inc(rows_free, 1)

            sp.sem_inc(rows_free, 2)
            with sp.Fori(0, NU // 2 - 1) as q:
                free_rows(Step(q, 0))
                free_rows(Step(q, 1))
            sp.wait_ge(count_ready, 1)
            for e in range(E):
                n_rows = sp.value_load(count_i[0:1, e:e + 1], min_val=0, max_val=TOK)
                sp.dma_start(sorted_rows[ds(n_rows + e * REGION, P), :], pad_rows[:, e, :]).then_inc(pads_in, 16)
            sp.wait_ge(pads_in, 16 * (E + SPARE))
            for i in range(2):
                sp.wait_ge(scattered[i], 16 * SCATTERS * (NU // 2))
            sp.wait_ge(table_ready, 1)

            def load_rows(q, b):
                s = q * RING + b
                at_least(sp, y_out[b], q * 16)
                first = sp.value_load(slot_row[0:1, ds(s, 1)], min_val=0, max_val=E * REGION + (SPARE - 1) * P)
                sp.dma_start(xs[b][:], sorted_rows[ds(first, P), :]).then_inc(xs_in[b], 16)

            for b in range(RING):
                load_rows(0, b)
            with sp.Fori(1, NS // RING) as q:
                for b in range(RING):
                    load_rows(q, b)
            for b in range(NS % RING):
                load_rows(NS // RING, b)

            for b in range(RING):
                sp.wait_ge(y_out[b], 16 * ((NS - b + RING - 1) // RING))

            def load_results(u):
                at_least(sp, res_ready, u.n - 1)
                for k, y in ((0, y0), (1, y1)):
                    src = result_rows[ds(u.n * TPU * P + k * TOK, TPU * P), :]
                    sp.dma_start(y[u.par][:].rearrange("p (b m) -> p b m", b=2),
                                 src.rearrange("(b p s) c -> p b (s c)", p=P, s=2)).then_inc(y_in[u.par], 16)

            load_results(Step(0, 0))
            load_results(Step(0, 1))
            with sp.Fori(1, NU // 2) as q:
                load_results(Step(q, 0))
                load_results(Step(q, 1))

        @block.tensor
        def _(pe):
            def weights_product():
                nc.tensor.transpose(bank[4][0:DIM, 0:P], wq[:], ident[:]).then_inc(wq_t_ps, 1)
                pe.wait_ge(wq_t_sb, 1)
                nc.tensor.matmul(bank[5][:, 0:C], wq_t[:], wr[:], start=True, stop=True).then_inc(wqr_ps, 1)
                pe.wait_ge(bq_wide_ready, 1)
                nc.tensor.matmul(bank[6][:, 0:C], bq_wide[:], wr[:], start=True, stop=True).then_inc(wqr_ps, 1)

            def transpose_xn(u):
                pe.wait_ge(xn_ready, u.n + 1)
                at_least(pe, xnt_sb, u.n)
                for t in range(TPU):
                    last = nc.tensor.transpose(bank[0][:, t * P:(t + 1) * P], xn[u.par][:, t, :], ident[:])
                last.then_inc(xnt_ps, 1)

            def project_kv(u):
                pe.wait_ge(xnt_sb, u.n + 1)
                at_least(pe, exp_done, u.n)
                nc.tensor.matmul(bank[1][:], wkv[:], xn_t[:], start=True, stop=True).then_inc(kv_ps, 1)

            def transpose_probs(u):
                wait_in_front(pe, waited_pe, (probs_ready, u.n + 1), *([(pk_sb, u.n)] if units.has(u.shift(-1)) else []))
                for t in range(TPU):
                    last = nc.tensor.transpose(bank[2][:, t * VDIM:(t + 1) * VDIM],
                                               probs[u.par][0:VDIM, t // 2, (t % 2) * P:(t % 2 + 1) * P],
                                               ident[0:VDIM, 0:VDIM])
                last.then_inc(pk_ps, 1)

            def weigh_tokens(u):
                pe.wait_ge(pk_sb, u.n + 1)
                at_least(pe, mix_sb, u.n)
                for m in range(2):
                    for s in range(2):
                        last = nc.tensor.matmul(bank[3][:, m * VDIM:(m + 1) * VDIM], xn[u.par][:, 2 * m + s, :],
                                                pk[:, 2 * m + s, :], start=(s == 0), stop=(s == 1))
                last.then_inc(xk_ps, 1)

            def mix_channels(u):
                pe.wait_ge(xk_sb, u.n + 1)
                at_least(pe, wqr_sb, 2)
                for m in range(2):
                    last = nc.tensor.matmul(bank[3][VDIM:P, P + m * C:P + (m + 1) * C],
                                            xk[:, m * VDIM:(m + 1) * VDIM], wqr[:], start=True, stop=True)
                last.then_inc(mix_ps, 1)

            def attend(u):
                pe.wait_ge(mix_sb, u.n + 1)
                at_least(pe, x1_ready, u.n)
                for t in range(TPU):
                    m, s = t // 2, t % 2
                    o = bank[4][:, t * C:(t + 1) * C]
                    last = nc.tensor.matmul(o, probs[u.par][VDIM:P, m, s * P:(s + 1) * P],
                                            mix[VDIM:P, m * C:(m + 1) * C], start=True, stop=True)
                last.then_inc(attn_ps, 1)

            def transpose_tn(u):
                pe.wait_ge(tn_ready, u.n + 1)
                at_least(pe, tnt_sb, u.n)
                for t in range(TPU):
                    last = nc.tensor.transpose(bank[5][:, t * P:(t + 1) * P], row_buf[u.par][:, t, 0, 0:C], ident[:])
                last.then_inc(tnt_ps, 1)

            def route(u):
                pe.wait_ge(tnt_sb, u.n + 1)
                at_least(pe, rows_ready, u.n)
                for t in range(TPU):
                    last = nc.tensor.matmul(bank[6][:, t * E:(t + 1) * E], tn_t[:, t * P:(t + 1) * P], wg[:],
                                            start=True, stop=True)
                last.then_inc(logits_ps, 1)

            def rank(u):
                pe.wait_ge(member_ready, u.n + 1)
                o = bank[7]
                nc.tensor.matmul(o[:, 0:TPU * E], earlier[:], member[:].rearrange("p t e -> p (t e)"),
                                 start=True, stop=False)
                nc.tensor.matmul(o[:, 0:TPU * E].rearrange("p (t e) -> p t e", e=E), all_ones[:],
                                 seen[:].unsqueeze(1).broadcast_to([P, TPU, E]), start=False, stop=False)
                for t in range(TPU - 1):
                    rest = TPU - 1 - t
                    last = nc.tensor.matmul(o[:, (t + 1) * E:TPU * E].rearrange("p (t e) -> p t e", e=E), all_ones[:],
                                            member[:, t:t + 1, :].broadcast_to([P, rest, E]),
                                            start=False, stop=(rest == 1))
                last.then_inc(rank_ps, 1)

            def iteration(i):
                new, old = i.shift(1), i.shift(-1)
                if units.has(i):
                    transpose_probs(i)
                    weigh_tokens(i)
                    mix_channels(i)
                    attend(i)
                if units.has(new):
                    transpose_xn(new)
                if units.has(old):
                    transpose_tn(old)
                if units.has(new):
                    project_kv(new)
                if units.has(old):
                    route(old)
                    rank(old)

            pe.wait_ge(small_in, 16 * 9)
            pe.wait_ge(pool_consts, POOL_CONSTS)
            weights_product()
            run_units(pe, iteration)
            pe.wait_ge(rows_ready, NU)
            nc.tensor.matmul(bank[7][:, 0:E], all_ones[:], seen[:], start=True, stop=True).then_inc(counts_ps, 1)

            pe.wait_ge(table_ready, 1)
            pe.wait_ge(expert_in, 64)

            def transpose_rows(s, b):
                pe.wait_ge(xs_in[b], 16 * s.round + 16)
                at_least(pe, xst_sb, s.n)
                nc.tensor.transpose(bank[0][:, 0:P], xs[b][:, 0:P], ident[:]).then_inc(xst_ps, 1)

            def up(s):
                e = pe.value_load(slot_expert[0:1, ds(s.n, 1)], min_val=0, max_val=E - 1)
                pe.wait_ge(xst_sb, s.n + 1)
                at_least(pe, silu_ready, s.n - 1)
                w = w1[:, ds(e, 1), :].rearrange("p a f -> p (a f)")
                nc.tensor.matmul(bank[1 + s.par][:, 0:F], xs_t[s.par][:], w, start=True, stop=True).then_inc(h_ps, 1)
                at_least(pe, gate_ready, s.n - 1)
                w = w3[:, ds(e, 1), :].rearrange("p a f -> p (a f)")
                nc.tensor.matmul(bank[3 + s.par][:, 0:F], xs_t[s.par][:], w, start=True, stop=True).then_inc(g_ps, 1)

            def transpose_act(s):
                pe.wait_ge(act_ready, s.n + 1)
                at_least(pe, actt_sb, s.n - 1)
                for k in range(KF):
                    last = nc.tensor.transpose(bank[5 + s.par][:, k * P:(k + 1) * P],
                                               act_rows[s.par][:, k * P:(k + 1) * P], ident[:])
                last.then_inc(actt_ps, 1)

            def down(s):
                e = pe.value_load(slot_expert[0:1, ds(s.n, 1)], min_val=0, max_val=E - 1)
                pe.wait_ge(actt_sb, s.n + 1)
                at_least(pe, y_sb, s.n)
                for k in range(KF):
                    last = nc.tensor.matmul(bank[7][:, 0:C], act_t[s.par][:, k * P:(k + 1) * P],
                                            w2[:, ds(e, 1), k, :].rearrange("p a c -> p (a c)"),
                                            start=(k == 0), stop=(k == KF - 1))
                last.then_inc(y_ps, 1)

            def step(s):
                if s.has(1):
                    transpose_rows(s.shift(1), s.shift(1).ring)
                if s.has(0):
                    up(s)
                if s.has(-1):
                    transpose_act(s.shift(-1))
                if s.has(-2):
                    down(s.shift(-2))

            run_slots(pe, step, lambda s: transpose_rows(s, 0))

        @block.scalar
        def _(act):
            for dst, src in ((wkv[:, 0:VDIM], Wk), (wkv[:, VDIM:P], Wv), (wq[:], Wq), (wr[:], Wr), (wg[:], Wg),
                             (bkv[0:VDIM, :], bk.unsqueeze(1)), (bkv[VDIM:P, :], bv.unsqueeze(1)),
                             (bq_col[:], bq.unsqueeze(1)), (br_all[:], br.partition_broadcast(P))):
                act.dma_start(dst, src).then_inc(small_in, 16)

            def copy_products():
                act.wait_ge(wq_t_ps, 1)
                nc.scalar.activation(wq_t[:], bank[4][0:DIM, 0:P], ACT.Copy).then_inc(wq_t_sb, 1)
                act.wait_ge(wqr_ps, 2)
                nc.scalar.activation(wqr[:], bank[5][:, 0:C], ACT.Copy).then_inc(wqr_sb, 1)
                nc.scalar.activation(bqr[:], bank[6][:, 0:C], ACT.Copy).then_inc(wqr_sb, 1)

            def normalise_x(u):
                act.wait_ge(shift_ready, u.n + 1)
                at_least(act, xk_ps, u.n - 1)
                for t in range(TPU):
                    last = nc.scalar.activation(xn[u.par][:, t, :],
                                                x_all[:, ds(u.n * TPU + t, 1), :].rearrange("p a c -> p (a c)"),
                                                ACT.Identity, bias=shift[:, 0, t:t + 1], scale=rstd[:, 0, t:t + 1])
                last.then_inc(xn_ready, 1)

            def copy_xnt(u):
                act.wait_ge(xnt_ps, u.n + 1)
                at_least(act, kv_ps, u.n)
                nc.scalar.activation(xn_t[:], bank[0][:], ACT.Copy).then_inc(xnt_sb, 1)

            def exp_kv(u):
                act.wait_ge(kv_bias, u.n + 1)
                at_least(act, probs_ready, u.n)
                for m in range(2):
                    last = nc.scalar.activation(exps[:, m, :], bank[1][:, m * IMG:(m + 1) * IMG], ACT.Exp,
                                                bias=exp_bias[:, m:m + 1], accum_out=exp_sum[:, m:m + 1])
                last.then_inc(exp_done, 1)

            def copy_pk(u):
                act.wait_ge(pk_ps, u.n + 1)
                at_least(act, xk_ps, u.n)
                nc.scalar.activation(pk[:], bank[2][:, 0:TPU * VDIM].rearrange("p (t v) -> p t v", t=TPU),
                                     ACT.Copy).then_inc(pk_sb, 1)

            def copy_xk(u):
                act.wait_ge(xk_ps, u.n + 1)
                at_least(act, mix_ps, u.n)
                nc.scalar.activation(xk[:], bank[3][:, 0:P], ACT.Copy).then_inc(xk_sb, 1)

            def normalise_t(u):
                act.wait_ge(shift_ready, u.n + 3)
                act.wait_ge(rows_free, u.n + 1)
                for t in range(TPU):
                    last = nc.scalar.activation(
                        row_buf[u.par][:, t, :, 0:C],
                        x1_all[:, ds(u.n * TPU + t, 1), :].broadcast_to([P, K, C]),
                        ACT.Identity, bias=shift[:, 1, t:t + 1], scale=rstd[:, 1, t:t + 1])
                last.then_inc(tn_ready, 1)

            def copy_tnt(u):
                act.wait_ge(tnt_ps, u.n + 1)
                at_least(act, logits_ps, u.n)
                nc.scalar.activation(tn_t[:], bank[5][:], ACT.Copy).then_inc(tnt_sb, 1)

            def exp_gap(u):
                act.wait_ge(gap_ready, u.n + 1)
                nc.scalar.activation(gap_exp[:], gap[:], ACT.Exp).then_inc(gap_exp_ready, 1)

            def iteration(i):
                new, old = i.shift(1), i.shift(-1)
                if units.has(i):
                    copy_pk(i)
                    copy_xk(i)
                if units.has(new):
                    normalise_x(new)
                if units.has(old):
                    normalise_t(old)
                if units.has(new):
                    copy_xnt(new)
                if units.has(old):
                    copy_tnt(old)
                if units.has(new):
                    exp_kv(new)
                if units.has(old):
                    exp_gap(old)

            copy_products()
            run_units(act, iteration)

            def copy_rows_t(s):
                act.wait_ge(xst_ps, s.n + 1)
                at_least(act, g_ps, s.n - 1)
                nc.scalar.activation(xs_t[s.par][:], bank[0][:, 0:P], ACT.Copy).then_inc(xst_sb, 1)

            def silu(s):
                act.wait_ge(h_ps, s.n + 1)
                at_least(act, act_ready, s.n - 1)
                nc.scalar.activation(silu_h[s.par][:], bank[1 + s.par][:, 0:F], ACT.Silu).then_inc(silu_ready, 1)

            def copy_act_t(s):
                act.wait_ge(actt_ps, s.n + 1)
                at_least(act, y_ps, s.n - 1)
                nc.scalar.activation(act_t[s.par][:], bank[5 + s.par][:, 0:F], ACT.Copy).then_inc(actt_sb, 1)

            def scale_result(s):
                act.wait_ge(y_ps, s.n + 1)
                at_least(act, y_out[s.ring], s.round * 16)
                nc.scalar.activation(ys[s.ring][:], bank[7][:, 0:C], ACT.Copy,
                                     scale=xs[s.ring][:, WEIGHT:WEIGHT + 1]).then_inc(y_sb, 1)

            def step(s):
                if s.has(1):
                    copy_rows_t(s.shift(1))
                if s.has(-2):
                    copy_act_t(s.shift(-2))
                if s.has(0):
                    silu(s)
                if s.has(-2):
                    scale_result(s.shift(-2))

            run_slots(act, step, copy_rows_t)

            def store(u):
                act.wait_ge(res_ready, u.n + 1)
                act.dma_start(out_tok[:, ds(u.n * 2, 2), :],
                              res[u.par][:].rearrange("p (b m) -> p b m", b=2)).then_inc(out_done[u.par], 16)

            with act.Fori(0, NU // 2) as q:
                store(Step(q, 0))
                store(Step(q, 1))
            for i in range(2):
                act.wait_ge(out_done[i], 16 * (NU // 2))

        @block.vector
        def _(dve):
            nc.vector.memset(eps[:, 0], LN_C_EPS)
            nc.vector.memset(eps[:, 1], LN_T_EPS)
            nc.vector.memset(power[:], -0.5)
            nc.vector.memset(mean_var[:], 0.0)
            nc.vector.memset(seen[:], 0.0)
            nc.vector.memset(all_ones[:], 1.0).then_inc(dve_consts, 1)
            dve.wait_ge(pool_consts, POOL_CONSTS)
            nc.vector.tensor_copy(iota_e[:], iota_ei[:])
            nc.vector.tensor_copy(region[:], region_i[:])
            nc.vector.tensor_copy(iota_s[:], iota_si[:]).then_inc(dve_consts, 1)

            def after(ins, semaphore, value):
                ins.then_inc(semaphore, 1)
                dve.wait_ge(semaphore, value)

            def stats_of_x(u):
                wait_in_front(dve, waited_dve, (x_in[u.par], u.half * 16 + 16))
                for t in range(TPU):
                    last = nc.vector.bn_stats(stats[:, 0, t, :],
                                              x_all[:, ds(u.n * TPU + t, 1), :].rearrange("p a c -> p (a c)"))
                last.then_inc(bn_c_steps, 1)
                wait_in_front(dve, waited_dve, (bn_c_steps, u.n * 2 + 1), *units.read(u.n))
                for t in range(TPU):
                    last = nc.vector.bn_aggr(mean_var[:, 0, t, :], stats[:, 0, t, :])
                last.then_inc(bn_c_steps, 1)

            def stats_of_x1(u):
                wait_in_front(dve, waited_dve, (x1_ready, u.n + 1))
                for t in range(TPU):
                    last = nc.vector.bn_stats(stats[:, 1, t, :],
                                              x1_all[:, ds(u.n * TPU + t, 1), :].rearrange("p a c -> p (a c)"))
                last.then_inc(bn_t_steps, 1)
                wait_in_front(dve, waited_dve, (bn_t_steps, u.n * 2 + 1), *units.read(u.n + 2))
                for t in range(TPU):
                    last = nc.vector.bn_aggr(mean_var[:, 1, t, :], stats[:, 1, t, :])
                last.then_inc(bn_t_steps, 1)

            def find_shift(m):
                dve.wait_ge(rstd_ready, m.n + 1)
                at_least(dve, xn_ready, units.upto(m.n))
                at_least(dve, tn_ready, m.n - 2)
                nc.vector.scalar_tensor_tensor(out=shift[:], in0=mean_var[:, :, :, 0], scalar=-1.0, in1=rstd[:],
                                               op0=ALU.mult, op1=ALU.mult).then_inc(shift_ready, 1)

            def add_br(u):
                nc.vector.tensor_tensor(x1_all[:, ds(u.n * TPU, TPU), :], x_all[:, ds(u.n * TPU, TPU), :],
                                        br_all[:].unsqueeze(1).broadcast_to([P, TPU, C]),
                                        ALU.add).then_inc(x_br_ready, 1)

            def add_mix_bias(u):
                dve.wait_ge(mix_ps, u.n + 1)
                at_least(dve, attn_ps, u.n)
                nc.vector.tensor_tensor(mix[VDIM:P, :].rearrange("p (m c) -> p m c", m=2),
                                        bank[3][VDIM:P, P:P + 2 * C].rearrange("p (m c) -> p m c", m=2),
                                        bqr[VDIM:P, :].unsqueeze(1).broadcast_to([VDIM, 2, C]),
                                        ALU.add).then_inc(mix_sb, 1)

            def max_kv(u):
                dve.wait_ge(kv_ps, u.n + 1)
                after(nc.vector.tensor_reduce(col_max[:], bank[1][:].rearrange("p (m n) -> p m n", m=2), AX.X,
                                              ALU.max), max_steps, u.n * 2 + 1)
                after(nc.vector.tensor_scalar(neg_max[:], col_max[:], bkv[:, 0:1], -1.0, ALU.add, ALU.mult),
                      max_steps, u.n * 2 + 2)
                nc.vector.tensor_scalar(exp_bias[:], neg_max[:], bkv[:, 0:1], None, ALU.add).then_inc(kv_bias, 1)

            def normalise_probs(u):
                dve.wait_ge(exp_done, u.n + 1)
                after(nc.vector.reciprocal(inv_sum[:], exp_sum[:]), sum_steps, u.n + 1)
                at_least(dve, attn_ps, u.n - 1)
                for m in range(2):
                    last = nc.vector.tensor_scalar(probs[u.par][:, m, :], exps[:, m, :], inv_sum[:, m:m + 1], None, ALU.mult)
                last.then_inc(probs_ready, 1)

            def add_x(u):
                dve.wait_ge(attn_ps, u.n + 1)
                dve.wait_ge(x_br_ready, u.n + 1)
                nc.vector.tensor_tensor(x1_all[:, ds(u.n * TPU, TPU), :],
                                        bank[4][:].rearrange("p (t c) -> p t c", t=TPU),
                                        x1_all[:, ds(u.n * TPU, TPU), :], ALU.add).then_inc(x1_ready, 1)

            def choose(u):
                wait_in_front(dve, waited_dve, (logits_ps, u.n + 1))
                for t in range(TPU):
                    last = nc.vector.max(top[:, t, :], bank[6][:, t * E:(t + 1) * E])
                after(last, pick_steps, u.n * 3 + 1)
                nc.vector.tensor_tensor(gap[:], top[:, :, 1], top[:, :, 0], ALU.subtract).then_inc(gap_ready, 1)
                for t in range(TPU):
                    last = nc.vector.max_index(top_idx[:, t, :], top[:, t, :], bank[6][:, t * E:(t + 1) * E])
                after(last, pick_steps, u.n * 3 + 2)
                after(nc.vector.tensor_tensor(
                    chosen[:], iota_e[:].unsqueeze(1).unsqueeze(1).broadcast_to([P, K, TPU, E]),
                    top_idx[:, :, 0:K].rearrange("p t k -> p k t").unsqueeze(3).broadcast_to([P, K, TPU, E]),
                    ALU.is_equal), pick_steps, u.n * 3 + 3)
                nc.vector.tensor_tensor(member[:], chosen[:, 0], chosen[:, 1], ALU.add).then_inc(member_ready, 1)

            def weigh_and_place(u):
                rows_i = row_buf[u.par][:].bitcast(I32)
                dve.wait_ge(rows_free, u.n + 1)
                nc.vector.tensor_copy(rows_i[:, :, :, DEST], dest_ids[:, ds(u.n * TPU, TPU), :])
                dve.wait_ge(gap_exp_ready, u.n + 1)
                after(nc.vector.tensor_scalar(gap_den[:], gap_exp[:], 1.0, None, ALU.add), weight_steps, u.n * 2 + 1)
                after(nc.vector.reciprocal(row_buf[u.par][:, :, 0, WEIGHT], gap_den[:]), weight_steps, u.n * 2 + 2)
                nc.vector.tensor_tensor(row_buf[u.par][:, :, 1, WEIGHT], gap_exp[:], row_buf[u.par][:, :, 0, WEIGHT],
                                        ALU.mult)
                dve.wait_ge(rank_ps, u.n + 1)
                after(nc.vector.tensor_tensor(place[:], bank[7][:, 0:TPU * E].rearrange("p (t e) -> p t e", e=E),
                                              region[:].unsqueeze(1).broadcast_to([P, TPU, E]), ALU.add),
                      place_steps, u.n * 3 + 1)
                after(nc.vector.tensor_tensor(place_of[:].rearrange("p (k t) e -> p k t e", k=K), chosen[:],
                                              place[:].unsqueeze(1).broadcast_to([P, K, TPU, E]), ALU.mult),
                      place_steps, u.n * 3 + 2)
                with nc.allow_low_precision("whole numbers below 2^24, and sums of up to four ones"):
                    nc.vector.tensor_reduce(position[u.par][:], place_of[:], AX.X, ALU.add)
                    after(nc.vector.tensor_reduce(member_sum[:], member[:].rearrange("p t e -> p e t"), AX.X, ALU.add),
                          place_steps, u.n * 3 + 3)
                nc.vector.tensor_tensor(seen[:], seen[:], member_sum[:], ALU.add).then_inc(rows_ready, 1)

            def iteration(i):
                new, old = i.shift(1), i.shift(-1)
                find_shift(new)
                if units.has(i):
                    add_mix_bias(i)
                if units.has(i.shift(2)):
                    stats_of_x(i.shift(2))
                if units.has(i):
                    add_x(i)
                    stats_of_x1(i)
                if units.has(new):
                    add_br(new)
                    max_kv(new)
                if units.has(old):
                    choose(old)
                if units.has(new):
                    normalise_probs(new)
                if units.has(old):
                    weigh_and_place(old)

            dve.wait_ge(small_in, 16 * 9)
            nc.vector.tensor_copy(bq_wide[:], bq_col[:].broadcast_to([DIM, P])).then_inc(bq_wide_ready, 1)
            stats_of_x(Step(0, 0))
            dve.wait_ge(wqr_sb, 2)
            run_units(dve, iteration)

            chain = [0]

            def link(ins):
                chain[0] += 1
                after(ins, table_steps, chain[0])

            dve.wait_ge(counts_ps, 1)
            nc.vector.tensor_copy(count_i[:], bank[7][0:1, 0:E]).then_inc(count_ready, 1)
            link(nc.vector.tensor_scalar(count_up[:], bank[7][0:1, 0:E], float(P - 1), None, ALU.add))
            link(nc.vector.tensor_single_scalar(tiles_i[:], count_up[:], P.bit_length() - 1, ALU.arith_shift_right))
            link(nc.vector.tensor_copy(tiles_f[:], tiles_i[:]))
            run = tiles_f
            for i in range(E.bit_length() - 1):
                d = 1 << i
                nc.vector.tensor_copy(ends[i][:, 0:d], run[:, 0:d])
                link(nc.vector.tensor_tensor(ends[i][:, d:E], run[:, d:E], run[:, 0:E - d], ALU.add))
                run = ends[i]
            link(nc.vector.tensor_tensor(past[:], run[:].unsqueeze(1).broadcast_to([1, NS, E]),
                                         iota_s[:].unsqueeze(2).broadcast_to([1, NS, E]), ALU.is_le))
            nc.vector.tensor_reduce(slot_e[:], past[:], AX.X, ALU.add)
            link(nc.vector.tensor_tensor(past_tiles[:], past[:], tiles_f[:].unsqueeze(1).broadcast_to([1, NS, E]),
                                         ALU.mult))
            nc.vector.tensor_scalar(slot_expert[:], slot_e[:], float(E - 1), None, ALU.min)
            link(nc.vector.tensor_reduce(slot_first[:], past_tiles[:], AX.X, ALU.add))
            link(nc.vector.tensor_tensor(slot_in[:], iota_s[:], slot_first[:], ALU.subtract))
            link(nc.vector.tensor_scalar(slot_base[:], slot_e[:], float(REGION), None, ALU.mult))
            nc.vector.scalar_tensor_tensor(out=slot_row[:], in0=slot_in[:], scalar=float(P), in1=slot_base[:],
                                           op0=ALU.mult, op1=ALU.add).then_inc(table_ready, 1)
            dve.wait_ge(table_ready, 1)
            dve.wait_ge(expert_in, 64)

            def gated(s):
                e = dve.value_load(slot_expert[0:1, ds(s.n, 1)], min_val=0, max_val=E - 1)
                dve.wait_ge(g_ps, s.n + 1)
                nc.vector.tensor_tensor(gate[s.par][:], bank[3 + s.par][:, 0:F],
                                        b3_all[:, ds(e, 1), :].rearrange("p a f -> p (a f)"),
                                        ALU.add).then_inc(gate_ready, 1)
                dve.wait_ge(gate_ready, s.n + 1)
                dve.wait_ge(silu_ready, s.n + 1)
                at_least(dve, actt_ps, s.n - 1)
                nc.vector.tensor_tensor(act_rows[s.par][:], silu_h[s.par][:], gate[s.par][:],
                                        ALU.mult).then_inc(act_ready, 1)

            def step(s):
                if s.has(0):
                    gated(s)

            run_slots(dve, step)

            def combine(u):
                dve.wait_ge(y_in[u.par], u.half * 32 + 32)
                nc.vector.tensor_tensor(half_sum[u.par][:], y0[u.par][:], y1[u.par][:], ALU.add).then_inc(half_ready, 1)
                dve.wait_ge(half_ready, u.n + 1)
                at_least(dve, out_done[u.par], u.half * 16)
                nc.vector.tensor_tensor(res[u.par][:], half_sum[u.par][:],
                                        x1_all[:, ds(u.n * TPU, TPU), :].rearrange("p t c -> p (t c)"),
                                        ALU.add).then_inc(res_ready, 1)

            combine(Step(0, 0))
            combine(Step(0, 1))
            with dve.Fori(1, NU // 2) as q:
                combine(Step(q, 0))
                combine(Step(q, 1))

        @block.gpsimd
        def _(pool):
            nc.gpsimd.memset(ident[:], 0.0)
            nc.gpsimd.memset(earlier[:], 1.0)
            nc.gpsimd.memset(pad_rows[:], 0.0).then_inc(pool_steps, 1)
            pool.wait_ge(pool_steps, 1)
            nc.gpsimd.affine_select(out=ident[:], in_=ident[:], compare_op=ALU.not_equal, fill=1.0, base=0,
                                    pattern=[[-1, P]], channel_multiplier=1).then_inc(pool_consts, 1)
            nc.gpsimd.affine_select(out=earlier[:], in_=earlier[:], compare_op=ALU.is_gt, fill=0.0, base=0,
                                    pattern=[[1, P]], channel_multiplier=-1).then_inc(pool_consts, 1)
            nc.gpsimd.iota(iota_ei[:], [[1, E]], base=0, channel_multiplier=0).then_inc(pool_consts, 1)
            nc.gpsimd.iota(region_i[:], [[REGION, E]], base=0, channel_multiplier=0).then_inc(pool_consts, 1)
            nc.gpsimd.iota(dest_ids[:].rearrange("p (b s) k -> p b s k", s=2), [[2 * P, NT // 2], [1, 2], [TOK, K]],
                           base=0, channel_multiplier=2).then_inc(pool_consts, 1)
            nc.gpsimd.iota(iota_si[:], [[1, NS]], base=0, channel_multiplier=0).then_inc(pool_consts, 1)
            nc.gpsimd.iota(pad_rows[:].bitcast(I32)[:, :, DEST], [[P, E + SPARE]], base=K * TOK,
                           channel_multiplier=1).then_inc(pool_consts, 1)

            def scatter_rows(u):
                wait_in_front(pool, waited_pool, (tn_ready, u.n + 1), (rows_ready, u.n + 1))
                for k in range(K):
                    for t in range(TPU):
                        c = k * TPU + t
                        nc.gpsimd.indirect_dma_start(
                            out=sorted_rows.ap(),
                            out_offset=bass.IndirectOffsetOnAxis(ap=position[u.par][:, c:c + 1], axis=0),
                            in_=row_buf[u.par][:, t, k, :], in_offset=None).then_inc(scattered[u.par], 16)

            def find_rstd(m):
                if units.has(m):
                    pool.wait_ge(bn_c_steps, m.n * 2 + 2)
                at_least(pool, bn_t_steps, (m.n - 1) * 2)
                at_least(pool, xn_ready, units.upto(m.n))
                at_least(pool, tn_ready, m.n - 2)
                nc.gpsimd.tensor_tensor(var_eps[:], mean_var[:, :, :, 1], eps[:], ALU.add).then_inc(power_steps, 1)
                pool.wait_ge(power_steps, m.n + 1)
                nc.gpsimd.tensor_tensor(rstd[:], var_eps[:], power[:], ALU.pow).then_inc(rstd_ready, 1)

            def iteration(i):
                find_rstd(i.shift(1))
                if units.has(i.shift(-2)):
                    scatter_rows(i.shift(-2))

            pool.wait_ge(dve_consts, 1)
            run_units(pool, iteration)
            scatter_rows(Step(0, NU - 1))

            def scatter_results(s):
                wait_in_front(pool, waited_pool, (y_sb, s.n + 1))
                nc.gpsimd.indirect_dma_start(
                    out=result_rows.ap(),
                    out_offset=bass.IndirectOffsetOnAxis(ap=xs[s.ring][:].bitcast(I32)[:, DEST:DEST + 1], axis=0),
                    in_=ys[s.ring][:], in_offset=None).then_inc(y_out[s.ring], 16)

            with pool.Fori(0, NS // RING) as q:
                for o in range(RING):
                    scatter_results(Slot(q, o, RING, NS))
            for n in range(NS // RING * RING, NS):
                scatter_results(Slot(0, n, RING, NS))


INPUTS = ("x", "L0_conv_Wq", "L0_conv_bq", "L0_conv_Wk", "L0_conv_bk", "L0_conv_Wv", "L0_conv_bv", "L0_conv_Wr",
          "L0_conv_br", "L0_ffn_Wg", "L0_ffn_W1", "L0_ffn_W2", "L0_ffn_W3", "L0_ffn_b3")


def kernel(**inputs):
    import numpy as np
    import concourse.bacc as bacc
    from concourse.bass_utils import run_bass_kernel_spmd

    nc = bacc.Bacc("TRN2", target_bir_lowering=False, num_devices=1)
    arrays, args = {}, []
    for name in INPUTS:
        a = np.ascontiguousarray(inputs[name])
        arrays[f"{name}_dram"] = a
        args.append(nc.dram_tensor(f"{name}_dram", a.shape, mybir.dt.from_np(a.dtype), kind="ExternalInput").ap())
    out = nc.dram_tensor("out_dram", inputs["x"].shape, F32, kind="ExternalOutput").ap()
    build(nc, *args, out)
    got = run_bass_kernel_spmd(nc, [arrays], core_ids=[0])
    return got.results[0]["out_dram"]
```

```python
from contextlib import ExitStack

import concourse.bass as bass
from concourse import mybir

F32 = mybir.dt.float32
F32R = mybir.dt.float32r
BF16 = mybir.dt.bfloat16
I32 = mybir.dt.int32
U32 = mybir.dt.uint32
ALU = mybir.AluOpType
ACT = mybir.ActivationFunctionType
AX = mybir.AxisListType

P = 128
LN_C_EPS = 1e-6
LN_T_EPS = 1e-5


def ds(start, size):
    return slice(start, start + size) if isinstance(start, int) else bass.ds(start, size)


class Step:

    def __init__(self, pair, offset):
        self.pair, self.offset = pair, offset
        self.par = offset % 2
        self.half = pair + offset // 2
        self.n = pair * 2 + offset

    def shift(self, k):
        return Step(self.pair, self.offset + k)


class Slot:

    def __init__(self, rnd, offset, ring, tiles):
        self.rnd, self.offset, self.size, self.tiles = rnd, offset, ring, tiles
        self.n = rnd * ring + offset
        self.par = offset % 2
        self.ring = offset % ring
        self.round = rnd + offset // ring

    def shift(self, k):
        return Slot(self.rnd, self.offset + k, self.size, self.tiles)

    def has(self, k):
        return not isinstance(self.n, int) or 0 <= self.n + k < self.tiles


def build(nc, x, Wq, bq, Wk, bk, Wv, bv, Wr, br, Wg, W1, W2, W3, b3, out):
    B, H, W, C = x.shape
    TOK = B * H * W
    NT = TOK // P
    DIM = Wq.shape[1]
    VDIM = Wk.shape[1]
    E, _, F = W1.shape
    TPU = 4
    NU = NT // TPU
    IMG = H * W
    K = 2
    KF = F // P
    REGION = TOK + P
    NS = (K * TOK + E * (P - 1)) // P
    SPARE = NS - K * TOK // P
    LOOPED = NU - 4
    ROW = P + 2
    RING = 8
    LAST_RING = 4
    DEST, WEIGHT = P, P + 1
    assert IMG == 2 * P and C == P and 2 * DIM == P and 2 * VDIM == P and NU % 2 == 0
    assert E == NU

    x_tok = x.rearrange("b h w c -> (b h w) c").rearrange("(b p s) c -> p b (s c)", p=P, s=2)
    out_tok = out.rearrange("b h w c -> (b h w) c").rearrange("(b p s) c -> p b (s c)", p=P, s=2)

    sorted_rows = nc.dram_tensor("sorted_rows", [E * REGION + SPARE * P, ROW], F32)
    result_rows = nc.dram_tensor("result_rows", [K * TOK + (E + SPARE) * P, P], F32)

    with ExitStack() as ctx:
        def sb(name, shape, dt=F32):
            return ctx.enter_context(nc.sbuf_tensor(name, shape, dt))

        def sem(name):
            return ctx.enter_context(nc.semaphore(name))

        bank = [ctx.enter_context(nc.psum_tensor(f"bank{i}", [P, 512], F32)) for i in range(8)]

        ident = sb("ident", [P, P])
        earlier = sb("earlier", [P, P], BF16)
        all_ones = sb("all_ones", [P, P], BF16)
        iota_e = sb("iota_e", [P, E])
        iota_ei = sb("iota_ei", [P, E], I32)
        region_i = sb("region_i", [P, E], I32)
        region = sb("region", [P, E])
        dest_ids = sb("dest_ids", [P, NT, K], I32)
        iota_s = sb("iota_s", [1, NS])
        iota_si = sb("iota_si", [1, NS], I32)
        eps = sb("eps", [P, 2, TPU])
        pad_rows = sb("pad_rows", [P, E + SPARE, ROW])

        wkv = sb("wkv", [P, P])
        bkv = sb("bkv", [P, 1])
        wq = sb("wq", [P, DIM])
        bq_col = sb("bq_col", [DIM, 1])
        wr = sb("wr", [DIM, C])
        br_all = sb("br_all", [P, C])
        wq_t = sb("wq_t", [DIM, C])
        wqr = sb("wqr", [P, C])
        bq_wide = sb("bq_wide", [DIM, P])
        bqr = sb("bqr", [P, C])
        wg = sb("wg", [P, E])
        w_all = sb("w_all", [P, E, 3, F])
        w_up = sb("w_up", [P, E, 2, 2, F], F32R)
        w_down = sb("w_down", [P, E, KF, 2, C], F32R)
        b3_all = sb("b3_all", [P, E, F])

        x_all = sb("x_all", [P, NT, C])
        x1_all = x_all
        stats = sb("stats", [P, 2, TPU, 6])
        mean_var = sb("mean_var", [P, 2, TPU, 2])
        var_eps = sb("var_eps", [P, 2, TPU])
        power = sb("power", [P, 2, TPU])
        rstd = sb("rstd", [P, 2, TPU])
        shift = sb("shift", [P, 2, TPU])
        xn = [sb(f"xn{i}", [P, TPU, C]) for i in range(2)]
        xn_t = sb("xn_t", [P, TPU * P])
        col_max = sb("col_max", [P, 2])
        neg_max = sb("neg_max", [P, 2])
        exp_bias = sb("exp_bias", [P, 2])
        exps = sb("exps", [P, 2, IMG])
        exp_sum = sb("exp_sum", [P, 2])
        inv_sum = sb("inv_sum", [P, 2])
        probs = [sb(f"probs{i}", [P, 2, IMG]) for i in range(2)]
        pk = sb("pk", [P, TPU, VDIM])
        xk = sb("xk", [P, 2 * VDIM])
        mix = sb("mix", [P, 2 * C])
        row_buf = [sb(f"row_buf{i}", [P, TPU, K, ROW]) for i in range(2)]
        tn_t = sb("tn_t", [P, TPU * P])
        top = sb("top", [P, TPU, 8])
        top_idx = sb("top_idx", [P, TPU, 8], U32)
        swapped = sb("swapped", [P, TPU])
        chosen = sb("chosen", [P, K, TPU, E])
        member = sb("member", [P, TPU, E], BF16)
        member_sum = sb("member_sum", [P, E], BF16)
        seen = sb("seen", [P, E], BF16)
        gap = sb("gap", [P, TPU])
        gap_exp = sb("gap_exp", [P, TPU])
        gap_den = sb("gap_den", [P, TPU])
        warm = sb("warm", [1, 1])
        place = sb("place", [P, TPU, E])
        place_of = sb("place_of", [P, K * TPU, E])
        position = [sb(f"position{i}", [P, K * TPU], I32) for i in range(2)]

        count_i = sb("count_i", [1, E], I32)
        count_up = sb("count_up", [1, E], I32)
        tiles_i = sb("tiles_i", [1, E], I32)
        tiles_f = sb("tiles_f", [1, E])
        ends = [sb(f"ends{i}", [1, E]) for i in range(4)]
        past = sb("past", [1, NS, E])
        past_tiles = sb("past_tiles", [1, NS, E])
        slot_e = sb("slot_e", [1, NS])
        slot_first = sb("slot_first", [1, NS])
        slot_in = sb("slot_in", [1, NS])
        slot_base = sb("slot_base", [1, NS])
        slot_row = sb("slot_row", [1, NS], I32)
        slot_expert = sb("slot_expert", [1, NS], I32)
        ring_up = sb("ring_up", [1, RING])
        ring_upi = sb("ring_upi", [1, RING], I32)
        before_last = sb("before_last", [1, RING], I32)
        ring_tiles = sb("ring_tiles", [1, RING], I32)
        first_half = sb("first_half", [1, RING], I32)

        xs = [sb(f"xs{i}", [P, ROW]) for i in range(RING)]
        xs_hi = [sb(f"xs_hi{i}", [P, P], F32R) for i in range(2)]
        xs_lo = [sb(f"xs_lo{i}", [P, P], F32R) for i in range(2)]
        silu_h = [sb(f"silu_h{i}", [P, F]) for i in range(2)]
        gate = [sb(f"gate{i}", [P, F]) for i in range(2)]
        act_rows = [sb(f"act_rows{i}", [P, F]) for i in range(2)]
        act_hi = [sb(f"act_hi{i}", [P, F], F32R) for i in range(2)]
        act_lo = [sb(f"act_lo{i}", [P, F], F32R) for i in range(2)]
        w_flat = w_all[:].rearrange("p e j f -> p (e j f)")
        UC = TPU * C
        both = w_flat[:, 0:NU * K * UC]
        ys = [w_flat[:, NU * K * UC + i * P:NU * K * UC + (i + 1) * P] for i in range(RING)]
        assert NU * K * UC + RING * P <= E * 3 * F
        y_parts = [sb(f"y_parts{i}", [P, 2, C]) for i in range(2)]

        pool_consts = sem("pool_consts")
        dve_consts = sem("dve_consts")
        kv_in = sem("kv_in")
        small_in = sem("small_in")
        b3_in = sem("b3_in")
        expert_in = sem("expert_in")
        w_hi_ready = sem("w_hi_ready")
        w_lo_ready = sem("w_lo_ready")
        wq_t_ps = sem("wq_t_ps")
        wq_t_sb = sem("wq_t_sb")
        wqr_ps = sem("wqr_ps")
        wqr_sb = sem("wqr_sb")
        x_in = [sem(f"x_in{i}") for i in range(2)]
        rstd_ready = sem("rstd_ready")
        shift_ready = sem("shift_ready")
        x_br_ready = sem("x_br_ready")
        xn_ready = sem("xn_ready")
        xnt_ps = sem("xnt_ps")
        xnt_sb = sem("xnt_sb")
        kv_ps = sem("kv_ps")
        kv_bias = sem("kv_bias")
        exp_done = sem("exp_done")
        probs_ready = sem("probs_ready")
        pk_ps = sem("pk_ps")
        pk_sb = sem("pk_sb")
        xk_ps = sem("xk_ps")
        xk_sb = sem("xk_sb")
        mix_ps = sem("mix_ps")
        mix_sb = sem("mix_sb")
        attn_ps = sem("attn_ps")
        x1_ready = sem("x1_ready")
        tn_ready = sem("tn_ready")
        tnt_ps = sem("tnt_ps")
        tnt_sb = sem("tnt_sb")
        logits_ps = sem("logits_ps")
        member_ready = sem("member_ready")
        gap_ready = sem("gap_ready")
        gap_exp_ready = sem("gap_exp_ready")
        rank_ps = sem("rank_ps")
        rows_ready = sem("rows_ready")
        rows_free = sem("rows_free")
        scattered = [sem(f"scattered{i}") for i in range(2)]
        bn_c_steps = sem("bn_c_steps")
        bn_t_steps = sem("bn_t_steps")
        power_steps = sem("power_steps")
        bq_wide_ready = sem("bq_wide_ready")
        max_steps = sem("max_steps")
        sum_steps = sem("sum_steps")
        pick_steps = sem("pick_steps")
        weight_steps = sem("weight_steps")
        place_steps = sem("place_steps")
        table_steps = sem("table_steps")
        pool_steps = sem("pool_steps")
        waited_dve = sem("waited_dve")
        waited_pool = sem("waited_pool")
        waited_pe = sem("waited_pe")
        counts_ps = sem("counts_ps")
        count_ready = sem("count_ready")
        table_ready = sem("table_ready")
        half_table = sem("half_table")
        waited_sp = sem("waited_sp")
        pads_in = sem("pads_in")
        xs_in = [sem(f"xs_in{i}") for i in range(RING)]
        xst_ps = sem("xst_ps")
        xs_hi_ready = sem("xs_hi_ready")
        xs_lo_ready = sem("xs_lo_ready")
        h_ps = sem("h_ps")
        g_ps = sem("g_ps")
        silu_ready = sem("silu_ready")
        gate_ready = sem("gate_ready")
        act_ready = sem("act_ready")
        actt_ps = sem("actt_ps")
        act_hi_ready = sem("act_hi_ready")
        act_lo_ready = sem("act_lo_ready")
        y_ps = sem("y_ps")
        y_sb = sem("y_sb")
        y_sum = sem("y_sum")
        y_out = [sem(f"y_out{i}") for i in range(RING)]
        y_in = [[sem(f"y_in{i}_{k}") for k in range(K)] for i in range(LAST_RING)]
        half_ready = sem("half_ready")
        res_ready = sem("res_ready")
        out_done = sem("out_done")

        POOL_CONSTS = 8
        EXPERT_LOADS = 16 * (2 + KF)
        SCATTERS = K * TPU
        block = ctx.enter_context(nc.Block())

        def at_least(eng, semaphore, value):
            if not (isinstance(value, int) and value <= 0):
                eng.wait_ge(semaphore, value)

        def wait_in_front(eng, own, *waits):
            for semaphore, value in waits:
                eng.wait_ge(semaphore, value)
            eng.sem_inc(own, 1)

        def exists(u):
            return not isinstance(u.n, int) or 0 <= u.n < NU

        def mean_var_read(n):
            return [] if isinstance(n, int) and n <= 0 else [(rstd_ready, n), (shift_ready, n)]

        def wait_norms(eng, m):
            if exists(m.shift(-1)):
                eng.wait_ge(xn_ready, m.n)
            else:
                at_least(eng, tn_ready, m.n - 3)

        def run_units(eng, iteration, first=2):
            for i in range(-2, first):
                iteration(Step(0, i))
            with eng.Fori(1, 1 + LOOPED // 2) as q:
                iteration(Step(q, first - 2))
                iteration(Step(q, first - 1))
            for i in range(first + LOOPED, NU + 1):
                iteration(Step(0, i))

        def run_slots(eng, step, before=None):
            if before is not None:
                before(Slot(0, 0, RING, NS))
            rounds = (NS - 1) // RING
            for o in range(RING):
                step(Slot(0, o, RING, NS))
            with eng.Fori(1, rounds) as q:
                for o in range(RING):
                    step(Slot(q, o, RING, NS))
            for n in range(rounds * RING, NS + 2):
                step(Slot(0, n, RING, NS))

        def load_experts(s, experts, engine):
            back = 0 if isinstance(s.n, int) and s.n == 0 else 4
            ahead = min(RING, NS - s.n) if isinstance(s.n, int) else RING
            _, values = nc.values_load_multi_w_load_instructions(
                slot_expert[0:1, ds(s.n - back, back + ahead)], engines=(engine,), min_val=0, max_val=E - 1,
                skip_runtime_bounds_check_because="VectorE clamps slot_expert to 0 .. E-1 when it writes it")
            for i, value in enumerate(values):
                experts[s.offset - back + i] = value

        @block.sync
        def _(sp):
            def load_x(u):
                at_least(sp, x_in[u.par], u.half * 16)
                sp.dma_start(x_all[:, ds(u.n * TPU, TPU), :].rearrange("p (b s) c -> p b (s c)", s=2),
                             x_tok[:, ds(u.n * 2, 2), :]).then_inc(x_in[u.par], 16)

            load_x(Step(0, 0))
            for dst, src in ((wkv[:, 0:VDIM], Wk), (wkv[:, VDIM:P], Wv),
                             (bkv[0:VDIM, :], bk.unsqueeze(1)), (bkv[VDIM:P, :], bv.unsqueeze(1))):
                sp.dma_start(dst, src).then_inc(kv_in, 16)
            for u in range(1, 4):
                load_x(Step(0, u))
            sp.dma_start(w_all[:, :, 0, :], W1.rearrange("e c f -> c e f")).then_inc(expert_in, 16)
            sp.dma_start(w_all[:, :, 1, :], W3.rearrange("e c f -> c e f")).then_inc(expert_in, 16)
            for k in range(KF):
                sp.dma_start(w_all[:, :, 2, k * C:(k + 1) * C],
                             W2[:, k * P:(k + 1) * P, :].rearrange("e p d -> p e d")).then_inc(expert_in, 16)
            with sp.Fori(2, NU // 2) as q:
                load_x(Step(q, 0))
                load_x(Step(q, 1))
            sp.dma_start(b3_all[:].rearrange("p e f -> p (e f)"),
                         b3.rearrange("e f -> (e f)").partition_broadcast(P)).then_inc(b3_in, 16)
            sp.wait_ge(pool_consts, POOL_CONSTS)
            for i in range(SPARE):
                first = E * REGION + i * P
                sp.dma_start(sorted_rows[first:first + P, :], pad_rows[:, E + i, :]).then_inc(pads_in, 16)

            def free_rows(u):
                sp.wait_ge(scattered[u.par], u.half * (16 * SCATTERS) + 16 * SCATTERS)
                sp.sem_inc(rows_free, 1)

            sp.sem_inc(rows_free, 2)
            with sp.Fori(0, NU // 2 - 1) as q:
                free_rows(Step(q, 0))
                free_rows(Step(q, 1))
            sp.wait_ge(count_ready, 1)
            for e in range(E):
                n_rows = sp.value_load(count_i[0:1, e:e + 1], min_val=0, max_val=TOK)
                sp.dma_start(sorted_rows[ds(n_rows + e * REGION, P), :], pad_rows[:, e, :]).then_inc(pads_in, 16)
            sp.wait_ge(table_ready, 1)

            def load_rows(q, b):
                s = q * RING + b
                at_least(sp, y_out[b], q * 16)
                first = sp.value_load(slot_row[0:1, ds(s, 1)], min_val=0, max_val=E * REGION + (SPARE - 1) * P)
                if isinstance(s, int) and s == 0:
                    sp.wait_ge(pads_in, 16 * (E + SPARE))
                    for i in range(2):
                        sp.wait_ge(scattered[i], 16 * SCATTERS * (NU // 2))
                sp.dma_start(xs[b][:], sorted_rows[ds(first, P), :]).then_inc(xs_in[b], 16)

            for b in range(RING):
                load_rows(0, b)
            with sp.Fori(1, NS // RING) as q:
                for b in range(RING):
                    load_rows(q, b)
            for b in range(NS % RING):
                load_rows(NS // RING, b)

            def load_results(u, k):
                at_least(sp, y_in[u.ring][k], u.round * 16)
                src = result_rows[ds(u.n * TPU * P + k * TOK, TPU * P), :]
                sp.dma_start(both[:, ds((u.n * K + k) * UC, UC)].rearrange("p (b m) -> p b m", b=2),
                             src.rearrange("(b p s) c -> p b (s c)", p=P, s=2)).then_inc(y_in[u.ring][k], 16)

            def load_half(k):
                for o in range(LAST_RING):
                    load_results(Slot(0, o, LAST_RING, NU), k)
                with sp.Fori(1, NU // LAST_RING) as q:
                    for o in range(LAST_RING):
                        load_results(Slot(q, o, LAST_RING, NU), k)

            sp.wait_ge(half_table, 1)
            for b in range(RING):
                count = sp.value_load(first_half[0:1, b:b + 1], min_val=16, max_val=16 * ((NS + RING - 1) // RING))
                wait_in_front(sp, waited_sp, (y_out[b], count))
            load_half(0)
            for b in range(RING):
                sp.wait_ge(y_out[b], 16 * ((NS - b + RING - 1) // RING))
            load_half(1)

        @block.tensor
        def _(pe):
            def weights_product():
                pe.wait_ge(small_in, 16 * 5)
                nc.tensor.transpose(bank[4][0:DIM, 0:P], wq[:], ident[:]).then_inc(wq_t_ps, 1)
                pe.wait_ge(wq_t_sb, 1)
                nc.tensor.matmul(bank[5][:, 0:C], wq_t[:], wr[:], start=True, stop=True).then_inc(wqr_ps, 1)
                pe.wait_ge(bq_wide_ready, 1)
                nc.tensor.matmul(bank[5][:, C:2 * C], bq_wide[:], wr[:], start=True, stop=True).then_inc(wqr_ps, 1)

            def transpose_xn(u):
                pe.wait_ge(xn_ready, u.n + 1)
                at_least(pe, xnt_sb, u.n)
                for t in range(TPU):
                    last = nc.tensor.transpose(bank[0][:, t * P:(t + 1) * P], xn[u.par][:, t, :], ident[:])
                last.then_inc(xnt_ps, 1)

            def project_kv(u):
                pe.wait_ge(xnt_sb, u.n + 1)
                at_least(pe, exp_done, u.n)
                nc.tensor.matmul(bank[1][:], wkv[:], xn_t[:], start=True, stop=True).then_inc(kv_ps, 1)

            def transpose_probs(u):
                wait_in_front(pe, waited_pe, (probs_ready, u.n + 1), *([(pk_sb, u.n)] if exists(u.shift(-1)) else []))
                for t in range(TPU):
                    last = nc.tensor.transpose(bank[2][:, t * VDIM:(t + 1) * VDIM],
                                               probs[u.par][0:VDIM, t // 2, (t % 2) * P:(t % 2 + 1) * P],
                                               ident[0:VDIM, 0:VDIM])
                last.then_inc(pk_ps, 1)

            def weigh_tokens(u):
                pe.wait_ge(pk_sb, u.n + 1)
                at_least(pe, mix_sb, u.n)
                for m in range(2):
                    for s in range(2):
                        last = nc.tensor.matmul(bank[3][:, m * VDIM:(m + 1) * VDIM], xn[u.par][:, 2 * m + s, :],
                                                pk[:, 2 * m + s, :], start=(s == 0), stop=(s == 1))
                last.then_inc(xk_ps, 1)

            def mix_channels(u):
                pe.wait_ge(xk_sb, u.n + 1)
                at_least(pe, wqr_sb, 2)
                for m in range(2):
                    last = nc.tensor.matmul(bank[3][VDIM:P, P + m * C:P + (m + 1) * C],
                                            xk[:, m * VDIM:(m + 1) * VDIM], wqr[:], start=True, stop=True)
                last.then_inc(mix_ps, 1)

            def attend(u):
                pe.wait_ge(mix_sb, u.n + 1)
                at_least(pe, x1_ready, u.n)
                for t in range(TPU):
                    m, s = t // 2, t % 2
                    o = bank[4][:, t * C:(t + 1) * C]
                    last = nc.tensor.matmul(o, probs[u.par][VDIM:P, m, s * P:(s + 1) * P],
                                            mix[VDIM:P, m * C:(m + 1) * C], start=True, stop=True)
                last.then_inc(attn_ps, 1)

            def transpose_tn(u):
                pe.wait_ge(tn_ready, u.n + 1)
                at_least(pe, tnt_sb, u.n)
                for t in range(TPU):
                    last = nc.tensor.transpose(bank[5][:, t * P:(t + 1) * P], row_buf[u.par][:, t, 0, 0:C], ident[:])
                last.then_inc(tnt_ps, 1)

            def route(u):
                pe.wait_ge(tnt_sb, u.n + 1)
                at_least(pe, rows_ready, u.n)
                for t in range(TPU):
                    last = nc.tensor.matmul(bank[6][:, t * E:(t + 1) * E], tn_t[:, t * P:(t + 1) * P], wg[:],
                                            start=True, stop=True)
                last.then_inc(logits_ps, 1)

            def rank(u):
                pe.wait_ge(member_ready, u.n + 1)
                o = bank[7]
                nc.tensor.matmul(o[:, 0:TPU * E], earlier[:], member[:].rearrange("p t e -> p (t e)"),
                                 start=True, stop=False)
                nc.tensor.matmul(o[:, 0:TPU * E].rearrange("p (t e) -> p t e", e=E), all_ones[:],
                                 seen[:].unsqueeze(1).broadcast_to([P, TPU, E]), start=False, stop=False)
                for t in range(TPU - 1):
                    rest = TPU - 1 - t
                    last = nc.tensor.matmul(o[:, (t + 1) * E:TPU * E].rearrange("p (t e) -> p t e", e=E), all_ones[:],
                                            member[:, t:t + 1, :].broadcast_to([P, rest, E]),
                                            start=False, stop=(rest == 1))
                last.then_inc(rank_ps, 1)

            def keep_busy(free_bank, n):
                for _ in range(n):
                    nc.tensor.matmul(bank[free_bank][:].rearrange("p (a b) -> p a b", a=4), all_ones[:],
                                     all_ones[:].unsqueeze(1).broadcast_to([P, 4, P]), start=True, stop=True)

            def iteration(i):
                new, old = i.shift(1), i.shift(-1)
                keep_busy(7, 3)
                if exists(new):
                    transpose_xn(new)
                keep_busy(7, 1)
                if exists(i):
                    transpose_probs(i)
                keep_busy(7, 1)
                if exists(i.shift(-2)):
                    rank(i.shift(-2))
                keep_busy(6, 1)
                if exists(new):
                    project_kv(new)
                if isinstance(i.n, int) and i.n == -1:
                    weights_product()
                keep_busy(6, 2)
                if exists(i):
                    weigh_tokens(i)
                    keep_busy(6, 2)
                    mix_channels(i)
                keep_busy(6, 3)
                if exists(old):
                    transpose_tn(old)
                keep_busy(6, 1)
                if exists(i):
                    attend(i)
                keep_busy(6, 3)
                if exists(old):
                    route(old)

            pe.wait_ge(dve_consts, 2)
            pe.wait_ge(pool_consts, POOL_CONSTS)
            pe.wait_ge(kv_in, 16 * 4)
            run_units(pe, iteration)
            rank(Step(0, NU - 1))
            pe.wait_ge(rows_ready, NU)
            nc.tensor.matmul(bank[7][:, 0:E], all_ones[:], seen[:], start=True, stop=True).then_inc(counts_ps, 1)

            pe.wait_ge(table_ready, 1)
            pe.wait_ge(w_lo_ready, E)
            keep_busy(7, 24)

            def transpose_rows(s):
                at_least(pe, xs_lo_ready, s.n)
                pe.wait_ge(xs_in[s.ring], 16 * s.round + 16)
                nc.tensor.transpose(bank[0][:, 0:P], xs[s.ring][:, 0:P], ident[:]).then_inc(xst_ps, 1)

            def up(s, e):
                if not s.has(1):
                    pe.wait_ge(xs_lo_ready, s.n + 1)
                for j in range(2):
                    w = [w_up[:, ds(e, 1), j, half, :].rearrange("p a f -> p (a f)") for half in range(2)]
                    o = bank[1 + 2 * j + s.par][:, 0:F]
                    nc.tensor.matmul(o, xs_hi[s.par][:], w[0], start=True, stop=False)
                    nc.tensor.matmul(o, xs_lo[s.par][:], w[0], start=False, stop=False)
                    nc.tensor.matmul(o, xs_hi[s.par][:], w[1], start=False, stop=True).then_inc((h_ps, g_ps)[j], 1)

            def transpose_act(s):
                pe.wait_ge(act_ready, s.n + 1)
                for k in range(KF):
                    last = nc.tensor.transpose(bank[5 + s.par][:, k * P:(k + 1) * P],
                                               act_rows[s.par][:, k * P:(k + 1) * P], ident[:])
                last.then_inc(actt_ps, 1)

            def down(s, e):
                pe.wait_ge(act_lo_ready, s.n + 1)
                at_least(pe, y_sb, s.n)
                for k in range(KF):
                    w = w_down[:, ds(e, 1), k, :, :].rearrange("p a h c -> p (a h c)")
                    nc.tensor.matmul(bank[7][:, 0:2 * C], act_hi[s.par][:, k * P:(k + 1) * P], w,
                                     start=(k == 0), stop=False)
                    last = nc.tensor.matmul(bank[7][:, 0:C], act_lo[s.par][:, k * P:(k + 1) * P], w[:, 0:C],
                                            start=False, stop=(k == KF - 1))
                last.then_inc(y_ps, 1)

            experts = {}

            def step(s):
                if s.has(1):
                    transpose_rows(s.shift(1))
                if s.has(0):
                    if s.ring == 0:
                        load_experts(s, experts, mybir.EngineType.PE)
                    up(s, experts[s.offset])
                if s.has(-1):
                    transpose_act(s.shift(-1))
                if s.has(-2):
                    down(s.shift(-2), experts[s.offset - 2])

            run_slots(pe, step, transpose_rows)

        @block.scalar
        def _(act):
            for dst, src in ((wq[:], Wq), (wr[:], Wr), (bq_col[:], bq.unsqueeze(1)),
                             (br_all[:], br.partition_broadcast(P)), (wg[:], Wg)):
                act.dma_start(dst, src).then_inc(small_in, 16)

            def copy_products():
                act.wait_ge(wq_t_ps, 1)
                nc.scalar.activation(wq_t[:], bank[4][0:DIM, 0:P], ACT.Copy).then_inc(wq_t_sb, 1)
                act.wait_ge(wqr_ps, 2)
                nc.scalar.activation(wqr[:], bank[5][:, 0:C], ACT.Copy).then_inc(wqr_sb, 1)
                nc.scalar.activation(bqr[:], bank[5][:, C:2 * C], ACT.Copy).then_inc(wqr_sb, 1)

            def normalise_x(u):
                act.wait_ge(shift_ready, u.n + 1)
                at_least(act, xk_ps, u.n - 1)
                for t in range(TPU):
                    last = nc.scalar.activation(xn[u.par][:, t, :],
                                                x_all[:, ds(u.n * TPU + t, 1), :].rearrange("p a c -> p (a c)"),
                                                ACT.Identity, bias=shift[:, 0, t:t + 1], scale=rstd[:, 0, t:t + 1])
                last.then_inc(xn_ready, 1)

            def copy_xnt(u):
                act.wait_ge(xnt_ps, u.n + 1)
                at_least(act, kv_ps, u.n)
                nc.scalar.activation(xn_t[:], bank[0][:], ACT.Copy).then_inc(xnt_sb, 1)

            def exp_kv(u):
                act.wait_ge(kv_bias, u.n + 1)
                at_least(act, probs_ready, u.n)
                for m in range(2):
                    last = nc.scalar.activation(exps[:, m, :], bank[1][:, m * IMG:(m + 1) * IMG], ACT.Exp,
                                                bias=exp_bias[:, m:m + 1], accum_out=exp_sum[:, m:m + 1])
                last.then_inc(exp_done, 1)

            def copy_pk(u):
                act.wait_ge(pk_ps, u.n + 1)
                at_least(act, xk_ps, u.n)
                nc.scalar.activation(pk[:], bank[2][:, 0:TPU * VDIM].rearrange("p (t v) -> p t v", t=TPU),
                                     ACT.Copy).then_inc(pk_sb, 1)

            def copy_xk(u):
                act.wait_ge(xk_ps, u.n + 1)
                at_least(act, mix_ps, u.n)
                nc.scalar.activation(xk[:], bank[3][:, 0:P], ACT.Copy).then_inc(xk_sb, 1)

            def normalise_t(u):
                act.wait_ge(shift_ready, u.n + 4)
                act.wait_ge(rows_free, u.n + 1)
                normalise_tiles(u, range(TPU - 1))

            def normalise_tiles(u, tiles):
                for t in tiles:
                    last = nc.scalar.activation(
                        row_buf[u.par][:, t, :, 0:C],
                        x1_all[:, ds(u.n * TPU + t, 1), :].broadcast_to([P, K, C]),
                        ACT.Identity, bias=shift[:, 1, t:t + 1], scale=rstd[:, 1, t:t + 1])
                if TPU - 1 in tiles:
                    last.then_inc(tn_ready, 1)

            def copy_tnt(u):
                act.wait_ge(tnt_ps, u.n + 1)
                at_least(act, logits_ps, u.n)
                nc.scalar.activation(tn_t[:], bank[5][:], ACT.Copy).then_inc(tnt_sb, 1)

            def round_weights(u):
                act.wait_ge(expert_in, EXPERT_LOADS)
                nc.scalar.activation(w_up[:, ds(u.n, 1), :, 0, :].rearrange("p a j f -> p (a j) f"),
                                     w_all[:, ds(u.n, 1), 0:2, :].rearrange("p a j f -> p (a j) f"),
                                     ACT.Copy).then_inc(w_hi_ready, 1)
                nc.scalar.activation(w_down[:, ds(u.n, 1), :, 0, :].rearrange("p a k c -> p (a k) c"),
                                     w_all[:, ds(u.n, 1), 2, :].rearrange("p a (k c) -> p (a k) c", k=KF),
                                     ACT.Copy).then_inc(w_hi_ready, 1)

            def exp_gap(u):
                act.wait_ge(gap_ready, u.n + 1)
                nc.scalar.activation(gap_exp[:], gap[:], ACT.Exp).then_inc(gap_exp_ready, 1)

            def iteration(i):
                new, old = i.shift(1), i.shift(-1)
                if exists(new):
                    copy_xnt(new)
                if exists(i):
                    copy_pk(i)
                if exists(i.shift(-2)):
                    exp_gap(i.shift(-2))
                if exists(old):
                    normalise_t(old)
                if exists(i):
                    copy_xk(i)
                if exists(old):
                    normalise_tiles(old, [TPU - 1])
                first = isinstance(i.n, int) and i.n == -1
                if first:
                    normalise_x(i.shift(2))
                    copy_products()
                if exists(new):
                    exp_kv(new)
                if exists(old):
                    copy_tnt(old)
                if exists(i.shift(2)) and not first:
                    normalise_x(i.shift(2))
                if exists(i):
                    round_weights(i)

            run_units(act, iteration)
            exp_gap(Step(0, NU - 1))
            act.wait_ge(rows_ready, NU)
            nc.scalar.activation(warm[:], gap_exp[0:1, 0:1], ACT.Silu)

            def copy_rows_t(s):
                act.wait_ge(xst_ps, s.n + 1)
                at_least(act, g_ps, s.n - 1)
                at_least(act, xs_lo_ready, s.n - 1)
                nc.scalar.activation(xs_hi[s.par][:], bank[0][:, 0:P], ACT.Copy).then_inc(xs_hi_ready, 1)

            def silu(s):
                act.wait_ge(h_ps, s.n + 1)
                at_least(act, act_ready, s.n - 1)
                nc.scalar.activation(silu_h[s.par][:], bank[1 + s.par][:, 0:F], ACT.Silu).then_inc(silu_ready, 1)

            def copy_act_t(s):
                act.wait_ge(actt_ps, s.n + 1)
                at_least(act, y_ps, s.n - 1)
                nc.scalar.activation(act_hi[s.par][:], bank[5 + s.par][:, 0:F], ACT.Copy).then_inc(act_hi_ready, 1)

            def scale_result(s):
                act.wait_ge(y_ps, s.n + 1)
                at_least(act, y_sum, s.n - 1)
                nc.scalar.activation(y_parts[s.par][:].rearrange("p a c -> p (a c)"),
                                     bank[7][:, 0:2 * C], ACT.Copy,
                                     scale=xs[s.ring][:, WEIGHT:WEIGHT + 1]).then_inc(y_sb, 1)

            def step(s):
                if s.has(1):
                    copy_rows_t(s.shift(1))
                if s.has(0):
                    silu(s)
                if s.has(-1):
                    copy_act_t(s.shift(-1))
                if s.has(-2):
                    scale_result(s.shift(-2))

            run_slots(act, step, copy_rows_t)

            def store(u):
                act.wait_ge(res_ready, u.n + 1)
                act.dma_start(out_tok[:, ds(u.n * 2, 2), :],
                              both[:, ds((u.n * K + 1) * UC, UC)].rearrange("p (b m) -> p b m", b=2)
                              ).then_inc(out_done, 16)

            with act.Fori(0, NU // 2) as q:
                store(Step(q, 0))
                store(Step(q, 1))
            act.wait_ge(out_done, 16 * NU)

        @block.vector
        def _(dve):
            nc.vector.memset(eps[:, 0], LN_C_EPS)
            nc.vector.memset(eps[:, 1], LN_T_EPS)
            nc.vector.memset(power[:], -0.5)
            nc.vector.memset(mean_var[:], 0.0)
            nc.vector.memset(seen[:], 0.0)
            nc.vector.memset(all_ones[:], 1.0).then_inc(dve_consts, 1)
            dve.wait_ge(pool_consts, POOL_CONSTS)
            nc.vector.tensor_copy(iota_e[:], iota_ei[:])
            nc.vector.tensor_copy(region[:], region_i[:])
            nc.vector.tensor_copy(ring_up[:], ring_upi[:])
            nc.vector.tensor_copy(iota_s[:], iota_si[:]).then_inc(dve_consts, 1)

            def after(ins, semaphore, value):
                ins.then_inc(semaphore, 1)
                dve.wait_ge(semaphore, value)

            def stats_of_x(u):
                wait_in_front(dve, waited_dve, (x_in[u.par], u.half * 16 + 16))
                for t in range(TPU):
                    last = nc.vector.bn_stats(stats[:, 0, t, :],
                                              x_all[:, ds(u.n * TPU + t, 1), :].rearrange("p a c -> p (a c)"))
                last.then_inc(bn_c_steps, 1)
                wait_in_front(dve, waited_dve, (bn_c_steps, u.n * 2 + 1), *mean_var_read(u.n))
                for t in range(TPU):
                    last = nc.vector.bn_aggr(mean_var[:, 0, t, :], stats[:, 0, t, :])
                last.then_inc(bn_c_steps, 1)

            def stats_of_x1(u):
                wait_in_front(dve, waited_dve, (x1_ready, u.n + 1))
                for t in range(TPU):
                    last = nc.vector.bn_stats(stats[:, 1, t, :],
                                              x1_all[:, ds(u.n * TPU + t, 1), :].rearrange("p a c -> p (a c)"))
                last.then_inc(bn_t_steps, 1)
                wait_in_front(dve, waited_dve, (bn_t_steps, u.n * 2 + 1), *mean_var_read(u.n + 3))
                for t in range(TPU):
                    last = nc.vector.bn_aggr(mean_var[:, 1, t, :], stats[:, 1, t, :])
                last.then_inc(bn_t_steps, 1)

            def find_shift(m):
                dve.wait_ge(rstd_ready, m.n + 1)
                wait_norms(dve, m)
                nc.vector.scalar_tensor_tensor(out=shift[:], in0=mean_var[:, :, :, 0], scalar=-1.0, in1=rstd[:],
                                               op0=ALU.mult, op1=ALU.mult).then_inc(shift_ready, 1)

            def add_br(u):
                dve.wait_ge(xn_ready, u.n + 1)
                nc.vector.tensor_tensor(x1_all[:, ds(u.n * TPU, TPU), :], x_all[:, ds(u.n * TPU, TPU), :],
                                        br_all[:].unsqueeze(1).broadcast_to([P, TPU, C]),
                                        ALU.add).then_inc(x_br_ready, 1)

            def add_mix_bias(u):
                dve.wait_ge(mix_ps, u.n + 1)
                at_least(dve, attn_ps, u.n)
                nc.vector.tensor_tensor(mix[VDIM:P, :].rearrange("p (m c) -> p m c", m=2),
                                        bank[3][VDIM:P, P:P + 2 * C].rearrange("p (m c) -> p m c", m=2),
                                        bqr[VDIM:P, :].unsqueeze(1).broadcast_to([VDIM, 2, C]),
                                        ALU.add).then_inc(mix_sb, 1)

            def max_kv(u):
                dve.wait_ge(kv_ps, u.n + 1)
                after(nc.vector.tensor_reduce(col_max[:], bank[1][:].rearrange("p (m n) -> p m n", m=2), AX.X,
                                              ALU.max), max_steps, u.n * 2 + 1)
                after(nc.vector.tensor_scalar(neg_max[:], col_max[:], bkv[:, 0:1], -1.0, ALU.add, ALU.mult),
                      max_steps, u.n * 2 + 2)
                nc.vector.tensor_scalar(exp_bias[:], neg_max[:], bkv[:, 0:1], None, ALU.add).then_inc(kv_bias, 1)

            def normalise_probs(u):
                dve.wait_ge(exp_done, u.n + 1)
                after(nc.vector.reciprocal(inv_sum[:], exp_sum[:]), sum_steps, u.n + 1)
                at_least(dve, attn_ps, u.n - 1)
                for m in range(2):
                    last = nc.vector.tensor_scalar(probs[u.par][:, m, :], exps[:, m, :], inv_sum[:, m:m + 1], None, ALU.mult)
                last.then_inc(probs_ready, 1)

            def add_x(u):
                dve.wait_ge(attn_ps, u.n + 1)
                dve.wait_ge(x_br_ready, u.n + 1)
                nc.vector.tensor_tensor(x1_all[:, ds(u.n * TPU, TPU), :],
                                        bank[4][:].rearrange("p (t c) -> p t c", t=TPU),
                                        x1_all[:, ds(u.n * TPU, TPU), :], ALU.add).then_inc(x1_ready, 1)

            def choose(u):
                wait_in_front(dve, waited_dve, (logits_ps, u.n + 1))
                for t in range(TPU):
                    last = nc.vector.max(top[:, t, :], bank[6][:, t * E:(t + 1) * E])
                after(last, pick_steps, u.n * 3 + 1)
                nc.vector.tensor_tensor(gap[:], top[:, :, 1], top[:, :, 0], ALU.subtract).then_inc(gap_ready, 1)
                for t in range(TPU):
                    last = nc.vector.max_index(top_idx[:, t, :], top[:, t, :], bank[6][:, t * E:(t + 1) * E])
                after(last, pick_steps, u.n * 3 + 2)
                nc.vector.tensor_tensor(swapped[:], top_idx[:, :, 0], top_idx[:, :, 1], ALU.is_gt)
                after(nc.vector.tensor_tensor(
                    chosen[:], iota_e[:].unsqueeze(1).unsqueeze(1).broadcast_to([P, K, TPU, E]),
                    top_idx[:, :, 0:K].rearrange("p t k -> p k t").unsqueeze(3).broadcast_to([P, K, TPU, E]),
                    ALU.is_equal), pick_steps, u.n * 3 + 3)
                nc.vector.tensor_tensor(member[:], chosen[:, 0], chosen[:, 1], ALU.add).then_inc(member_ready, 1)

            def split_up_weights(u):
                dve.wait_ge(w_hi_ready, u.n * 2 + 2)
                nc.vector.tensor_tensor(w_up[:, ds(u.n, 1), :, 1, :].rearrange("p a j f -> p (a j) f"),
                                        w_all[:, ds(u.n, 1), 0:2, :].rearrange("p a j f -> p (a j) f"),
                                        w_up[:].bitcast(F32)[:, ds(u.n, 1), :, 0, :].rearrange("p a j f -> p (a j) f"),
                                        ALU.subtract)

            def split_down_weights(u):
                nc.vector.tensor_tensor(w_down[:, ds(u.n, 1), :, 1, :].rearrange("p a k c -> p (a k) c"),
                                        w_all[:, ds(u.n, 1), 2, :].rearrange("p a (k c) -> p (a k) c", k=KF),
                                        w_down[:].bitcast(F32)[:, ds(u.n, 1), :, 0, :].rearrange("p a k c -> p (a k) c"),
                                        ALU.subtract).then_inc(w_lo_ready, 1)

            def weigh_and_place(u):
                rows_i = row_buf[u.par][:].bitcast(I32)
                dve.wait_ge(rows_free, u.n + 1)
                for k, way in ((0, TOK), (1, -TOK)):
                    nc.vector.scalar_tensor_tensor(
                        out=rows_i[:, :, k, DEST], in0=swapped[:], scalar=float(way),
                        in1=dest_ids[:, ds(u.n * TPU, TPU), k], op0=ALU.mult, op1=ALU.add)
                dve.wait_ge(gap_exp_ready, u.n + 1)
                after(nc.vector.tensor_scalar(gap_den[:], gap_exp[:], 1.0, None, ALU.add), weight_steps, u.n * 2 + 1)
                after(nc.vector.reciprocal(row_buf[u.par][:, :, 0, WEIGHT], gap_den[:]), weight_steps, u.n * 2 + 2)
                nc.vector.tensor_tensor(row_buf[u.par][:, :, 1, WEIGHT], gap_exp[:], row_buf[u.par][:, :, 0, WEIGHT],
                                        ALU.mult)
                dve.wait_ge(rank_ps, u.n + 1)
                after(nc.vector.tensor_tensor(place[:], bank[7][:, 0:TPU * E].rearrange("p (t e) -> p t e", e=E),
                                              region[:].unsqueeze(1).broadcast_to([P, TPU, E]), ALU.add),
                      place_steps, u.n * 3 + 1)
                after(nc.vector.tensor_tensor(place_of[:].rearrange("p (k t) e -> p k t e", k=K), chosen[:],
                                              place[:].unsqueeze(1).broadcast_to([P, K, TPU, E]), ALU.mult),
                      place_steps, u.n * 3 + 2)
                with nc.allow_low_precision("whole numbers below 2^24, and sums of up to four ones"):
                    nc.vector.tensor_reduce(position[u.par][:], place_of[:], AX.X, ALU.add)
                    after(nc.vector.tensor_reduce(member_sum[:], member[:].rearrange("p t e -> p e t"), AX.X, ALU.add),
                          place_steps, u.n * 3 + 3)
                nc.vector.tensor_tensor(seen[:], seen[:], member_sum[:], ALU.add).then_inc(rows_ready, 1)

            def iteration(i):
                new, old = i.shift(1), i.shift(-1)
                if exists(new):
                    max_kv(new)
                if exists(old):
                    split_up_weights(old)
                if exists(i):
                    add_mix_bias(i)
                if exists(old):
                    split_down_weights(old)
                if exists(new):
                    normalise_probs(new)
                if exists(i.shift(3)):
                    stats_of_x(i.shift(3))
                if exists(i):
                    add_x(i)
                    stats_of_x1(i)
                if exists(old):
                    choose(old)
                if exists(i.shift(2)):
                    add_br(i.shift(2))
                if exists(old):
                    weigh_and_place(old)
                if not isinstance(i.n, int) or i.n < NU:
                    find_shift(i.shift(3))

            stats_of_x(Step(0, 0))
            find_shift(Step(0, 0))
            dve.wait_ge(small_in, 16 * 5)
            nc.vector.tensor_copy(bq_wide[:], bq_col[:].broadcast_to([DIM, P])).then_inc(bq_wide_ready, 1)
            dve.wait_ge(kv_in, 16 * 4)
            run_units(dve, iteration, first=1)

            chain = [0]

            def link(ins):
                chain[0] += 1
                after(ins, table_steps, chain[0])

            dve.wait_ge(counts_ps, 1)
            nc.vector.tensor_copy(count_i[:], bank[7][0:1, 0:E]).then_inc(count_ready, 1)
            link(nc.vector.tensor_scalar(count_up[:], bank[7][0:1, 0:E], float(P - 1), None, ALU.add))
            link(nc.vector.tensor_single_scalar(tiles_i[:], count_up[:], P.bit_length() - 1, ALU.arith_shift_right))
            link(nc.vector.tensor_copy(tiles_f[:], tiles_i[:]))
            run = tiles_f
            for i in range(E.bit_length() - 1):
                d = 1 << i
                nc.vector.tensor_copy(ends[i][:, 0:d], run[:, 0:d])
                link(nc.vector.tensor_tensor(ends[i][:, d:E], run[:, d:E], run[:, 0:E - d], ALU.add))
                run = ends[i]
            link(nc.vector.tensor_tensor(past[:], run[:].unsqueeze(1).broadcast_to([1, NS, E]),
                                         iota_s[:].unsqueeze(2).broadcast_to([1, NS, E]), ALU.is_le))
            nc.vector.tensor_reduce(slot_e[:], past[:], AX.X, ALU.add)
            link(nc.vector.tensor_tensor(past_tiles[:], past[:], tiles_f[:].unsqueeze(1).broadcast_to([1, NS, E]),
                                         ALU.mult))
            nc.vector.tensor_scalar(slot_expert[:], slot_e[:], float(E - 1), None, ALU.min)
            link(nc.vector.tensor_reduce(slot_first[:], past_tiles[:], AX.X, ALU.add))
            link(nc.vector.tensor_tensor(slot_in[:], iota_s[:], slot_first[:], ALU.subtract))
            link(nc.vector.tensor_scalar(slot_base[:], slot_e[:], float(REGION), None, ALU.mult))
            nc.vector.scalar_tensor_tensor(out=slot_row[:], in0=slot_in[:], scalar=float(P), in1=slot_base[:],
                                           op0=ALU.mult, op1=ALU.add).then_inc(table_ready, 1)
            link(nc.vector.tensor_tensor(before_last[:], ring_up[:], run[:, E - 2:E - 1].broadcast_to([1, RING]), ALU.add))
            link(nc.vector.tensor_single_scalar(ring_tiles[:], before_last[:], RING.bit_length() - 1,
                                                ALU.arith_shift_right))
            nc.vector.tensor_scalar(first_half[:], ring_tiles[:], 1.0, 16.0, ALU.max, ALU.mult).then_inc(half_table, 1)
            dve.wait_ge(table_ready, 1)
            dve.wait_ge(b3_in, 16)

            def add_b3(s, e):
                dve.wait_ge(g_ps, s.n + 1)
                nc.vector.tensor_tensor(gate[s.par][:], bank[3 + s.par][:, 0:F],
                                        b3_all[:, ds(e, 1), :].rearrange("p a f -> p (a f)"),
                                        ALU.add).then_inc(gate_ready, 1)

            def gated(s):
                dve.wait_ge(gate_ready, s.n + 1)
                dve.wait_ge(silu_ready, s.n + 1)
                at_least(dve, actt_ps, s.n - 1)
                nc.vector.tensor_tensor(act_rows[s.par][:], silu_h[s.par][:], gate[s.par][:],
                                        ALU.mult).then_inc(act_ready, 1)

            def split_rows(s):
                dve.wait_ge(xs_hi_ready, s.n + 1)
                at_least(dve, g_ps, s.n - 1)
                nc.vector.tensor_tensor(xs_lo[s.par][:], bank[0][:, 0:P], xs_hi[s.par][:].bitcast(F32),
                                        ALU.subtract).then_inc(xs_lo_ready, 1)

            def split_act(s):
                dve.wait_ge(act_hi_ready, s.n + 1)
                at_least(dve, y_ps, s.n - 1)
                nc.vector.tensor_tensor(act_lo[s.par][:], bank[5 + s.par][:, 0:F], act_hi[s.par][:].bitcast(F32),
                                        ALU.subtract).then_inc(act_lo_ready, 1)

            dve_experts = {}

            def step(s):
                if s.has(0):
                    if s.ring == 0:
                        load_experts(s, dve_experts, mybir.EngineType.DVE)
                if s.has(1):
                    split_rows(s.shift(1))
                if s.has(0):
                    add_b3(s, dve_experts[s.offset])
                    gated(s)
                if s.has(-1):
                    split_act(s.shift(-1))

            run_slots(dve, step, split_rows)

            def add_half(u, k, done):
                x1 = x1_all[:, ds(u.n * TPU, TPU), :].rearrange("p t c -> p (t c)")
                y = both[:, ds((u.n * K + k) * UC, UC)]
                dve.wait_ge(y_in[u.ring][k], u.round * 16 + 16)
                if k == 1:
                    dve.wait_ge(half_ready, NU)
                nc.vector.tensor_tensor(y if k == 1 else x1, x1, y, ALU.add).then_inc(done, 1)

            for k, done in ((0, half_ready), (1, res_ready)):
                with dve.Fori(0, NU // LAST_RING) as q:
                    for o in range(LAST_RING):
                        add_half(Slot(q, o, LAST_RING, NU), k, done)

        @block.gpsimd
        def _(pool):
            nc.gpsimd.memset(ident[:], 0.0)
            nc.gpsimd.memset(earlier[:], 1.0)
            nc.gpsimd.memset(pad_rows[:], 0.0).then_inc(pool_steps, 1)
            pool.wait_ge(pool_steps, 1)
            nc.gpsimd.affine_select(out=ident[:], in_=ident[:], compare_op=ALU.not_equal, fill=1.0, base=0,
                                    pattern=[[-1, P]], channel_multiplier=1).then_inc(pool_consts, 1)
            nc.gpsimd.affine_select(out=earlier[:], in_=earlier[:], compare_op=ALU.is_gt, fill=0.0, base=0,
                                    pattern=[[1, P]], channel_multiplier=-1).then_inc(pool_consts, 1)
            nc.gpsimd.iota(iota_ei[:], [[1, E]], base=0, channel_multiplier=0).then_inc(pool_consts, 1)
            nc.gpsimd.iota(region_i[:], [[REGION, E]], base=0, channel_multiplier=0).then_inc(pool_consts, 1)
            nc.gpsimd.iota(dest_ids[:].rearrange("p (b s) k -> p b s k", s=2), [[2 * P, NT // 2], [1, 2], [TOK, K]],
                           base=0, channel_multiplier=2).then_inc(pool_consts, 1)
            nc.gpsimd.iota(iota_si[:], [[1, NS]], base=0, channel_multiplier=0).then_inc(pool_consts, 1)
            nc.gpsimd.iota(ring_upi[:], [[-1, RING]], base=RING - 1, channel_multiplier=0).then_inc(pool_consts, 1)
            nc.gpsimd.iota(pad_rows[:].bitcast(I32)[:, :, DEST], [[P, E + SPARE]], base=K * TOK,
                           channel_multiplier=1).then_inc(pool_consts, 1)

            def scatter_rows(u):
                wait_in_front(pool, waited_pool, (tn_ready, u.n + 1), (rows_ready, u.n + 1))
                for k in range(K):
                    for t in range(TPU):
                        c = k * TPU + t
                        nc.gpsimd.indirect_dma_start(
                            out=sorted_rows.ap(),
                            out_offset=bass.IndirectOffsetOnAxis(ap=position[u.par][:, c:c + 1], axis=0),
                            in_=row_buf[u.par][:, t, k, :], in_offset=None).then_inc(scattered[u.par], 16)

            def find_rstd(m):
                if exists(m):
                    pool.wait_ge(bn_c_steps, m.n * 2 + 2)
                at_least(pool, bn_t_steps, (m.n - 2) * 2)
                at_least(pool, shift_ready, m.n)
                wait_norms(pool, m)
                nc.gpsimd.tensor_tensor(var_eps[:], mean_var[:, :, :, 1], eps[:], ALU.add).then_inc(power_steps, 1)
                pool.wait_ge(power_steps, m.n + 1)
                nc.gpsimd.tensor_tensor(rstd[:], var_eps[:], power[:], ALU.pow).then_inc(rstd_ready, 1)

            def iteration(i):
                find_rstd(i.shift(2))
                if exists(i.shift(-2)):
                    scatter_rows(i.shift(-2))

            pool.wait_ge(dve_consts, 1)
            run_units(pool, iteration)
            scatter_rows(Step(0, NU - 1))

            def scatter_results(s):
                pool.wait_ge(y_sb, s.n + 1)
                at_least(pool, y_out[s.ring], s.round * 16)
                nc.gpsimd.tensor_tensor(ys[s.ring][:], y_parts[s.par][:, 0, :], y_parts[s.par][:, 1, :],
                                        ALU.add).then_inc(y_sum, 1)
                wait_in_front(pool, waited_pool, (y_sum, s.n + 1))
                nc.gpsimd.indirect_dma_start(
                    out=result_rows.ap(),
                    out_offset=bass.IndirectOffsetOnAxis(ap=xs[s.ring][:].bitcast(I32)[:, DEST:DEST + 1], axis=0),
                    in_=ys[s.ring][:], in_offset=None).then_inc(y_out[s.ring], 16)

            for o in range(RING):
                scatter_results(Slot(0, o, RING, NS))
            with pool.Fori(1, NS // RING) as q:
                for o in range(RING):
                    scatter_results(Slot(q, o, RING, NS))
            for n in range(NS // RING * RING, NS):
                scatter_results(Slot(0, n, RING, NS))


INPUTS = ("x", "L0_conv_Wq", "L0_conv_bq", "L0_conv_Wk", "L0_conv_bk", "L0_conv_Wv", "L0_conv_bv", "L0_conv_Wr",
          "L0_conv_br", "L0_ffn_Wg", "L0_ffn_W1", "L0_ffn_W2", "L0_ffn_W3", "L0_ffn_b3")


def kernel(**inputs):
    import numpy as np
    import concourse.bacc as bacc
    from concourse.bass_utils import run_bass_kernel_spmd

    nc = bacc.Bacc("TRN2", target_bir_lowering=False, num_devices=1)
    arrays, args = {}, []
    for name in INPUTS:
        a = np.ascontiguousarray(inputs[name])
        arrays[f"{name}_dram"] = a
        args.append(nc.dram_tensor(f"{name}_dram", a.shape, mybir.dt.from_np(a.dtype), kind="ExternalInput").ap())
    out = nc.dram_tensor("out_dram", inputs["x"].shape, F32, kind="ExternalOutput").ap()
    build(nc, *args, out)
    got = run_bass_kernel_spmd(nc, [arrays], core_ids=[0])
    return got.results[0]["out_dram"]
```
